# Optimizing a Trainium2 kernel written in Bass

```python
import numpy as np
import jax
import jax.numpy as jnp

def _softmax(x, axis=-1):
    return jax.nn.softmax(x, axis=axis)

def _gelu(x):
    return jax.nn.gelu(x, approximate=True)

def _silu(x):
    return jax.nn.silu(x)

def _sigmoid(x):
    return jax.nn.sigmoid(x)

def _layernorm(x, axis=-1, eps=1e-05):
    m = jnp.mean(x, axis=axis, keepdims=True)
    v = jnp.var(x, axis=axis, keepdims=True)
    return (x - m) / jnp.sqrt(v + eps)

def _scatter_add(tgt, idx, src, axis=0):
    return tgt.at[idx].add(src)

def _segment_sum(src, seg, n):
    return jax.ops.segment_sum(src, seg, n)
kernel_name = 'mk_metaformer_d1_conv_nchw512_r4_78ee2f'

def setup_inputs(seed: int=0):
    np.random.seed(seed)
    _w = jnp.asarray

    def _rec_inputs():
        import jax
        import jax.numpy as jnp
        _gk = jax.random.key(seed)
        x = -7.109e-05 + 0.9999 * jax.random.normal(jax.random.fold_in(_gk, 1), (8, 128, 32, 32), jnp.float32)
        return x
    x = _rec_inputs()

    def _L0_conv_setup():
        import jax, jax.numpy as jnp
        import numpy as np
        B, C, H, W = (8, 128, 32, 32)
        WS = 8

        def _proj(x, w, b):
            return jnp.einsum('bchw,oc->bohw', x, w) + b[None, :, None, None]

        def _split_windows(x):
            b, c, h, w = x.shape
            x = x.reshape(b, c, h // WS, WS, w // WS, WS)
            x = x.transpose(0, 2, 4, 3, 5, 1)
            return x.reshape(-1, WS * WS, c)

        def _merge_windows(x, b, c, h, w):
            x = x.reshape(b, h // WS, w // WS, WS, WS, c)
            x = x.transpose(0, 5, 1, 3, 2, 4)
            return x.reshape(b, c, h, w)
        key = jax.random.key(seed)
        ks = jax.random.split(key, 9)
        s = 1.0 / np.sqrt(C)
        return {'x': jax.random.normal(ks[0], (B, C, H, W), jnp.float32), 'wq': jax.random.normal(ks[1], (C, C), jnp.float32) * s, 'bq': jnp.zeros((C,), jnp.float32), 'wk': jax.random.normal(ks[2], (C, C), jnp.float32) * s, 'bk': jnp.zeros((C,), jnp.float32), 'wv': jax.random.normal(ks[3], (C, C), jnp.float32) * s, 'bv': jnp.zeros((C,), jnp.float32), 'wo': jax.random.normal(ks[4], (C, C), jnp.float32) * s, 'bo': jnp.zeros((C,), jnp.float32)}
    _L0_conv_all = _L0_conv_setup()
    _L0_conv_in = {k: v for k, v in _L0_conv_all.items() if k in ('wq', 'bq', 'wk', 'bk', 'wv', 'bv', 'wo', 'bo')}
    del _L0_conv_all

    def _L0_ffn_setup():
        import jax, jax.numpy as jnp
        import numpy as np
        B, S, D = (8, 1024, 128)
        E, K, M = (16, 2, 256)
        key = jax.random.key(seed)
        ks = jax.random.split(key, 5)
        return {'x': jax.random.normal(ks[0], (B, S, D), dtype=jnp.float32), 'wg': jax.random.normal(ks[1], (D, E), dtype=jnp.float32) * D ** (-0.5), 'w0': jax.random.normal(ks[2], (E, D, M), dtype=jnp.float32) * D ** (-0.5), 'w1': jax.random.normal(ks[3], (E, D, M), dtype=jnp.float32) * D ** (-0.5), 'wo': jax.random.normal(ks[4], (E, M, D), dtype=jnp.float32) * M ** (-0.5)}
    _L0_ffn_all = _L0_ffn_setup()
    _L0_ffn_in = {k: v for k, v in _L0_ffn_all.items() if k in ('wg', 'w0', 'w1', 'wo')}
    del _L0_ffn_all
    return {'x': x, 'L0_conv_wq': _L0_conv_in['wq'], 'L0_conv_bq': _L0_conv_in['bq'], 'L0_conv_wk': _L0_conv_in['wk'], 'L0_conv_bk': _L0_conv_in['bk'], 'L0_conv_wv': _L0_conv_in['wv'], 'L0_conv_bv': _L0_conv_in['bv'], 'L0_conv_wo': _L0_conv_in['wo'], 'L0_conv_bo': _L0_conv_in['bo'], 'L0_ffn_wg': _L0_ffn_in['wg'], 'L0_ffn_w0': _L0_ffn_in['w0'], 'L0_ffn_w1': _L0_ffn_in['w1'], 'L0_ffn_wo': _L0_ffn_in['wo']}

def reference(x, L0_conv_wq, L0_conv_bq, L0_conv_wk, L0_conv_bk, L0_conv_wv, L0_conv_bv, L0_conv_wo, L0_conv_bo, L0_ffn_wg, L0_ffn_w0, L0_ffn_w1, L0_ffn_wo):
    import jax
    import jax.numpy as jnp

    def _L0_conv_ref(x, wq, bq, wk, bk, wv, bv, wo, bo):
        import jax, jax.numpy as jnp
        import numpy as np
        B, C, H, W = (8, 128, 32, 32)
        WS = 8

        def _proj(x, w, b):
            return jnp.einsum('bchw,oc->bohw', x, w) + b[None, :, None, None]

        def _split_windows(x):
            b, c, h, w = x.shape
            x = x.reshape(b, c, h // WS, WS, w // WS, WS)
            x = x.transpose(0, 2, 4, 3, 5, 1)
            return x.reshape(-1, WS * WS, c)

        def _merge_windows(x, b, c, h, w):
            x = x.reshape(b, h // WS, w // WS, WS, WS, c)
            x = x.transpose(0, 5, 1, 3, 2, 4)
            return x.reshape(b, c, h, w)
        b, c, h, w = x.shape
        q = _split_windows(_proj(x, wq, bq))
        k = _split_windows(_proj(x, wk, bk))
        v = _split_windows(_proj(x, wv, bv))
        attn = jnp.einsum('nqc,nkc->nqk', q, k) / jnp.sqrt(jnp.asarray(c, x.dtype))
        attn = jax.nn.softmax(attn, axis=-1)
        out = jnp.einsum('nqk,nkc->nqc', attn, v)
        out = _merge_windows(out, b, c, h, w)
        return _proj(out, wo, bo)

    def _L0_ffn_ref(x, wg, w0, w1, wo):
        import jax, jax.numpy as jnp
        import numpy as np
        B, S, D = (8, 1024, 128)
        E, K, M = (16, 2, 256)
        gate_logits = jnp.einsum('bsd,de->bse', x, wg)
        top_vals, top_idx = jax.lax.top_k(gate_logits, K)
        top_w = jax.nn.softmax(top_vals.astype(jnp.float32), axis=-1).astype(x.dtype)
        dense_w = jnp.sum(jax.nn.one_hot(top_idx, E, dtype=x.dtype) * top_w[..., None], axis=-2)
        out = jnp.zeros_like(x)
        for e in range(E):
            h = jax.nn.silu(x @ w0[e]) * (x @ w1[e])
            out = out + dense_w[..., e:e + 1] * (h @ wo[e])
        return out

    def _gn(v, G=32, eps=1e-05):
        B_, C_, H_, W_ = v.shape
        g = v.reshape(B_, G, C_ // G, H_, W_)
        m = jnp.mean(g, axis=(2, 3, 4), keepdims=True)
        s = jnp.var(g, axis=(2, 3, 4), keepdims=True)
        return ((g - m) / jnp.sqrt(s + eps)).reshape(v.shape)

    def _ln_c(v, eps=1e-06):
        m = jnp.mean(v, axis=1, keepdims=True)
        s = jnp.var(v, axis=1, keepdims=True)
        return (v - m) / jnp.sqrt(s + eps)

    def _ln_t(v, eps=1e-05):
        m = jnp.mean(v, axis=-1, keepdims=True)
        s = jnp.var(v, axis=-1, keepdims=True)
        return (v - m) / jnp.sqrt(s + eps)

    def _to_tokens(v):
        B_, C_, H_, W_ = v.shape
        return v.reshape(B_, C_, H_ * W_).transpose(0, 2, 1)

    def _from_tokens(t, like):
        B_, C_, H_, W_ = like.shape
        return t.transpose(0, 2, 1).reshape(B_, C_, H_, W_)
    x = x + _L0_conv_ref(_ln_c(x), L0_conv_wq, L0_conv_bq, L0_conv_wk, L0_conv_bk, L0_conv_wv, L0_conv_bv, L0_conv_wo, L0_conv_bo)
    t = _to_tokens(x)
    t = t + _L0_ffn_ref(_ln_t(t), L0_ffn_wg, L0_ffn_w0, L0_ffn_w1, L0_ffn_wo)
    x = _from_tokens(t, x)
    return x

_drawn_inputs = setup_inputs


def setup_inputs(seed=0):
    import zlib

    import numpy as np

    out = dict(_drawn_inputs(seed))
    spreads = {'L0_conv_bq': (0.0, 0.1),
     'L0_conv_bk': (0.0, 0.1),
     'L0_conv_bv': (0.0, 0.1),
     'L0_conv_bo': (0.0, 0.1)}
    factors = {}
    for name, (base, spread) in spreads.items():
        noise = np.random.default_rng([zlib.crc32(name.encode()), seed]).standard_normal(out[name].shape)
        drawn = base * np.exp(spread * noise) if base else spread * noise
        out[name] = jnp.asarray(drawn.astype(out[name].dtype))
    for name, factor in factors.items():
        out[name] = (out[name] * factor).astype(out[name].dtype)
    return out
```

```python
from contextlib import ExitStack

import concourse.bass as bass
from concourse import mybir

F32 = mybir.dt.float32
BF16 = mybir.dt.bfloat16
I32 = mybir.dt.int32
ALU = mybir.AluOpType
ACT = mybir.ActivationFunctionType
AX = mybir.AxisListType

P = 128
WS = 8
TPC = 4
CHUNK = TPC * P
RING = 4
SKEW = 3
LOWEST = -3.0e38


class Ticks:

    def __init__(self):
        self.base, self.count = 0, 0

    def up(self, n=1):
        self.count += n
        return self.base + self.count

    def now(self):
        return self.base + self.count


def emit(nc, x, wq, bq, wk, bk, wv, bv, wo, bo, wg, w0, w1, w2, out):
    B, C, H, W = x.shape
    E, D, M = w0.shape
    assert C == P and D == P and M == 2 * P and H * W % CHUNK == 0
    GROUPS = 2
    NCH = B * H * W // CHUNK // GROUPS
    NT = NCH * TPC
    PAIRS = 2 * NT * P
    TILES = -(-(PAIRS // P + E - 1) // RING) * RING
    ROUNDS = TILES // RING
    STEPS = NCH + SKEW - 1
    SPB = H * W // CHUNK
    SCALE = float(C) ** -0.5
    LN_C_EPS, LN_T_EPS = 1e-6, 1e-5

    tn_dram = [nc.dram_tensor(f"normed_{g}", (NT * P, D), F32, kind="Internal").ap() for g in range(GROUPS)]
    y_dram = [nc.dram_tensor(f"expert_rows_{g}", (TILES * P, D), F32, kind="Internal").ap() for g in range(GROUPS)]

    with ExitStack() as ctx:
        def sb(name, shape, dt=F32):
            return ctx.enter_context(nc.sbuf_tensor(name, shape, dt))

        def sem(name):
            return ctx.enter_context(nc.semaphore(name))

        ident = sb("ident", [P, P])
        ones_row = sb("ones_row", [1, P])
        ones_f = sb("ones_f", [P, P])
        ones_b = sb("ones_b", [P, P], BF16)
        before_b = sb("before_b", [P, P], BF16)
        earlier = sb("earlier", [P, E, E])
        rev_e = sb("rev_e", [P, TPC, E])
        part_col = sb("part_col", [P, 1])
        tile_row = sb("tile_row", [P, NT])
        iota_p = sb("iota_p", [P, P], BF16)
        iota_t = sb("iota_t", [P, TILES], BF16)
        iota_te = sb("iota_te", [P, TILES, E], BF16)
        raw = sb("raw", [P, 4, P])
        wqT = sb("wqT", [P, P])
        wkT = sb("wkT", [P, P])
        woT = sb("woT", [P, P])
        wvo = sb("wvo", [P, P])
        bcols = sb("bcols", [P, 3])
        bo_row = sb("bo_row", [1, P])
        bv_b = sb("bv_b", [P, P])
        bvo = sb("bvo", [P, P])
        wg_sb = sb("wg_sb", [P, E])
        w01 = sb("w01", [P, E, 2, M])
        w2_sb = sb("w2_sb", [P, E, 2, D])

        x_sb = sb("x_sb", [P, B * H * W // CHUNK, CHUNK])
        t_sb = sb("t_sb", [P, GROUPS * NT, D])
        xw = sb("xw", [P, CHUNK])
        tn_sb = sb("tn_sb", [P, TPC, D])
        oh = sb("oh", [P, 2, GROUPS * NT, E], BF16)
        gate = sb("gate", [P, 2, GROUPS * NT])
        rank = sb("rank", [P, NT, E])
        cum = sb("cum", [P, NT + 1, E], BF16)
        both = sb("both", [P, NT, E], BF16)

        st = sb("st", [P, TPC, 6])
        mv = sb("mv", [P, TPC, 2])
        rs = sb("rs", [P, TPC])
        nb = sb("nb", [P, TPC])
        var = sb("var", [P, TPC])
        bits = sb("bits", [P, TPC], I32)
        sq = sb("sq", [P, TPC])
        xn = sb("xn", [P, TPC, P])
        xnT = sb("xnT", [P, CHUNK])
        q_sb = sb("q_sb", [P, CHUNK])
        k_sb = sb("k_sb", [P, CHUNK])
        vo_sb = sb("vo_sb", [P, TPC, P])
        smax = sb("smax", [P, TPC])
        sc = sb("sc", [P, TPC, P // 2])
        prob = sb("prob", [P, TPC, P])
        pT = sb("pT", [P, CHUNK])
        den = sb("den", [P, TPC])
        st2 = sb("st2", [P, TPC, 6])
        mv2 = sb("mv2", [P, TPC, 2])
        rs2 = sb("rs2", [P, TPC])
        tnT = sb("tnT", [P, CHUNK])
        lg = sb("lg", [P, TPC, E])
        m1 = sb("m1", [P, TPC])
        m2 = sb("m2", [P, TPC])
        eq = sb("eq", [P, TPC, E])
        pick = sb("pick", [P, TPC])
        lg2 = sb("lg2", [P, TPC, E])
        dm = sb("dm", [P, 2, TPC])
        ex = sb("ex", [P, 2, TPC])
        tot = sb("tot", [P, E])
        tot_i = sb("tot_i", [P, E], I32)
        cnt_i = sb("cnt_i", [P, E], I32)
        ntile = sb("ntile", [P, E])
        prod = sb("prod", [P, E, E])
        first = sb("first", [P, E])
        base = sb("base", [P, E])
        ends = sb("ends", [P, E])
        done = sb("done", [P, TILES, E], BF16)
        exp_f = sb("exp_f", [P, TILES])
        exp_01 = sb("exp_01", [P, TILES], I32)
        exp_2 = sb("exp_2", [P, TILES], I32)
        place = sb("place", [P, NT, E])
        pp = sb("pp", [P, NT, E])
        slot = sb("slot", [P, 2, NT])
        slot_i = sb("slot_i", [P, GROUPS, 2, NT], I32)
        hi_i = sb("hi_i", [P, 2, NT], I32)
        lo_i = sb("lo_i", [P, 2, NT], I32)
        hi_f = sb("hi_f", [P, 2, NT])
        lo_f = sb("lo_f", [P, 2, NT])
        sel_p = sb("sel_p", [P, 2, P], BF16)
        sel_t = sb("sel_t", [P, 2, 2, TILES], BF16)
        lows = sb("lows", [P, TILES])
        src_f = sb("src_f", [P, TILES])
        src_i = sb("src_i", [P, TILES], I32)
        gidx = sb("gidx", [P, RING], I32)
        xg = sb("xg", [P, RING, D])
        xgT = sb("xgT", [P, 2, P])
        sil = sb("sil", [P, 2, M])
        hid = sb("hid", [P, 2, M])
        hT = sb("hT", [P, 2, M])
        ys = sb("ys", [P, 2, RING, D])
        cidx = sb("cidx", [P, 2, TPC], I32)
        yg = sb("yg", [P, 2, TPC, D])
        o1 = sb("o1", [P, TPC, D])
        o2 = sb("o2", [P, TPC, D])

        bank = [ctx.enter_context(nc.psum_tensor(f"bank{n}", [P, CHUNK], F32)) for n in range(8)]
        XT, XNT, Q, K, VO, S, PT, Y = bank
        LG, RK, DN = XNT[:, 0:64], XNT[:, 64:128], XNT[:, 128:132]
        TNT, OT = PT, XT

        def wait_apart(eng, *waits):
            waits = [(s, v if isinstance(v, int) else eng.to_reg(v)) for s, v in waits]
            eng.wait_ge(pool_c, NCONST)
            for s, v in waits:
                eng.wait_ge(s, v)

        def by_window(a):
            return a.rearrange("c a (s h w k) -> c (a s) w h k", h=WS, w=W // WS, k=WS)

        def by_tile(b):
            return b[:, :].rearrange("p (j n) -> p j n", j=TPC)

        NCONST = 14
        w_in = sem("w_in"); e_in = sem("e_in"); x_in = [sem(f"x_in{n}") for n in range(GROUPS + 2)]
        pool_c = sem("pool_c"); vec = sem("vec")
        wt_ps = sem("wt_ps"); wt_sb = sem("wt_sb"); wvo_ps = sem("wvo_ps"); wvo_sb = sem("wvo_sb")
        xt_ps = sem("xt_ps"); stats = sem("stats"); xn_ok = sem("xn_ok"); xb_ok = sem("xb_ok")
        xnt_ps = sem("xnt_ps"); xnt_ok = sem("xnt_ok")
        qkv_ps = sem("qkv_ps"); qkv_ok = sem("qkv_ok")
        s_ps = sem("s_ps"); sc_ok = sem("sc_ok"); p_ok = sem("p_ok")
        pt_ps = sem("pt_ps"); pt_ok = sem("pt_ok")
        y_ps = sem("y_ps"); t_ok = sem("t_ok"); den_ok = sem("den_ok"); tn_ok = sem("tn_ok")
        tnt_ps = sem("tnt_ps"); tnt_ok = sem("tnt_ok")
        lg_ps = sem("lg_ps"); lg_ok = sem("lg_ok"); dm_ok = sem("dm_ok"); ex_ok = sem("ex_ok")
        both_ok = sem("both_ok"); rk_ps = sem("rk_ps"); rk_ok = sem("rk_ok")
        tn_out = sem("tn_out")
        tot_ps = sem("tot_ps"); exp_ok = sem("exp_ok"); slots_ok = sem("slots_ok")
        sel_ok = sem("sel_ok"); sel_used = sem("sel_used"); src_ps = sem("src_ps"); src_ok = sem("src_ok")
        gidx_ok = sem("gidx_ok"); xg_in = [sem(f"xg_in{u}") for u in range(RING)]
        xgt_ps = sem("xgt_ps"); xgt_ok = sem("xgt_ok")
        h_ps = sem("h_ps"); sil_ok = sem("sil_ok"); hid_ok = sem("hid_ok")
        ht_ps = sem("ht_ps"); ht_ok = sem("ht_ok"); ye_ps = sem("ye_ps"); ye_ok = sem("ye_ok")
        y_out = sem("y_out")
        cidx_ok = sem("cidx_ok"); yg_in = [sem(f"yg_in{j}") for j in range(TPC)]
        o_ok = sem("o_ok"); ot_ps = sem("ot_ps"); ot_ok = sem("ot_ok"); ot_half = sem("ot_half"); x_win = sem("x_win"); o_out = sem("o_out")

        block = ctx.enter_context(nc.Block())

        def conv_steps(eng, g, step, ticks=None):
            before = g > 0
            lo, hi = SKEW - 1, NCH
            for i in range(lo):
                step(i, g * NCH + i, True, i >= 1, i >= 2, before and i >= 1)
            looped(eng, lo, hi, lambda i: step(i, g * NCH + i, True, True, True, before), ticks)
            for i in range(hi, STEPS):
                step(i, g * NCH + i, False, i - 1 < NCH, True, before and i - 1 < NCH)

        def looped(eng, lo, hi, body, ticks=None):
            if ticks is None:
                with eng.Fori(lo, hi) as i:
                    body(i)
                return
            ticks.base, ticks.count = ticks.now(), 0
            start = ticks.base
            body(lo)
            per = ticks.count
            with eng.Fori(lo + 1, hi) as i:
                ticks.base, ticks.count = (i - lo) * per + start, 0
                body(i)
                assert ticks.count == per
            ticks.base, ticks.count = start + per * (hi - lo), 0

        @block.sync
        def _(sp):
            x_v = x.rearrange("b c (s h) w -> c b s (h w)", s=SPB)
            x_s = x_sb[:, :, :].rearrange("c (b s) t -> c b s t", s=SPB)
            out_v = out.rearrange("b c (s h) w -> c b s (h w)", s=SPB)
            sp.dma_start(x_s[:, 0, 0, :], x_v[:, 0, 0, :]).then_inc(x_in[0], 16)
            for n, w in enumerate((wq, wk, wo, wv)):
                sp.dma_start(raw[:, n, :], w).then_inc(w_in, 16)
            sp.dma_start(bo_row[:, :], bo.rearrange("(a c) -> a c", a=1)).then_inc(w_in, 16)
            for n, b in enumerate((bq, bk, bv)):
                sp.dma_start(bcols[:, n:n + 1], b.rearrange("(c a) -> c a", a=1)).then_inc(w_in, 16)
            sp.dma_start(x_s[:, 0, 1:SPB, :], x_v[:, 0, 1:SPB, :]).then_inc(x_in[1], 16)
            sp.dma_start(wg_sb[:, :], wg).then_inc(w_in, 16)
            half = B // GROUPS
            sp.dma_start(x_s[:, 1:half, :, :].rearrange("c b s t -> c b (s t)"),
                         x_v[:, 1:half, :, :].rearrange("c b s t -> c b (s t)")).then_inc(x_in[2], 16)
            for g in range(1, GROUPS):
                sp.dma_start(x_s[:, g * half:(g + 1) * half, :, :].rearrange("c b s t -> c b (s t)"),
                             x_v[:, g * half:(g + 1) * half, :, :].rearrange("c b s t -> c b (s t)")
                             ).then_inc(x_in[g + 2], 16)
            sp.dma_start(w01[:, :, 0, :], w0.rearrange("e d m -> d e m")).then_inc(e_in, 16)
            sp.dma_start(w01[:, :, 1, :], w1.rearrange("e d m -> d e m")).then_inc(e_in, 16)
            sp.dma_start(w2_sb[:, :, :, :], w2.rearrange("e (k m) d -> m e k d", k=2)).then_inc(e_in, 16)

            def tn_store(g, n):
                sp.wait_ge(tn_ok, n + 1)
                rows = tn_dram[g].rearrange("(n j p) d -> p n j d", p=P, j=TPC)
                sp.dma_start(rows[:, bass.ds(n - g * NCH, 1), :, :], tn_sb[:, :, :].unsqueeze(1)).then_inc(tn_out, 16)

            def out_store(n):
                wait_apart(sp, (ot_ok, n + 1))
                sp.dma_start(out_v[:, bass.ds(n // SPB, 1), bass.ds(n % SPB, 1), :],
                             x_sb[:, bass.ds(n, 1), :].unsqueeze(1)).then_inc(o_out, 16)

            def step(g):
                def run(i, n, new, mid, old, back):
                    if mid:
                        tn_store(g, n - 1)
                    if back:
                        out_store(n - 1 - NCH)
                return run

            def y_store(g, r, half_ring):
                n = g * ROUNDS + r
                sp.wait_ge(ye_ok, (n + 1) * RING)
                rows = y_dram[g].rearrange("(r u p) d -> p r u d", p=P, u=RING)
                sp.dma_start(rows[:, bass.ds(r, 1), :, :], ys[:, half_ring:half_ring + 1, :, :]).then_inc(y_out, 16)
                wait_apart(sp, (y_out, (n + 1) * 16))

            for g in range(GROUPS):
                conv_steps(sp, g, step(g))

                def rounds(r2):
                    y_store(g, r2 * 2, 0)
                    y_store(g, r2 * 2 + 1, 1)
                looped(sp, 0, ROUNDS // 2, rounds)
            looped(sp, (GROUPS - 1) * NCH, GROUPS * NCH, out_store)
            sp.wait_ge(tn_out, GROUPS * NCH * 16)
            sp.wait_ge(y_out, GROUPS * ROUNDS * 16)
            sp.wait_ge(o_out, GROUPS * NCH * 16)

        @block.gpsimd
        def _(pool):
            made = Ticks()

            def make(ins):
                ins.then_inc(pool_c, 1)
                made.up()

            make(pool.memset(ident[:, :], 0.0))
            make(pool.memset(ones_f[:, :], 1.0))
            make(pool.memset(ones_b[:, :], 1.0))
            make(pool.memset(earlier[:, :, :], 1.0))
            make(pool.memset(ones_row[:, :], 1.0))
            make(pool.iota(rev_e[:, :, :], [[0, TPC], [-1, E]], base=E, channel_multiplier=0,
                           allow_small_or_imprecise_dtypes=True))
            make(pool.iota(part_col[:, :], [[0, 1]], base=0, channel_multiplier=1,
                           allow_small_or_imprecise_dtypes=True))
            make(pool.iota(tile_row[:, :], [[1, NT]], base=0, channel_multiplier=0,
                           allow_small_or_imprecise_dtypes=True))
            make(pool.iota(iota_p[:, :], [[1, P]], base=0, channel_multiplier=0,
                           allow_small_or_imprecise_dtypes=True))
            make(pool.iota(iota_t[:, :], [[1, TILES]], base=0, channel_multiplier=0,
                           allow_small_or_imprecise_dtypes=True))
            make(pool.iota(iota_te[:, :, :], [[1, TILES], [0, E]], base=0, channel_multiplier=0,
                           allow_small_or_imprecise_dtypes=True))
            pool.wait_ge(pool_c, made.now())
            make(pool.affine_select(out=ident[:, :], in_=ident[:, :], compare_op=ALU.not_equal, fill=1.0,
                                    base=0, pattern=[[-1, P]], channel_multiplier=1))
            make(pool.affine_select(out=before_b[:, :], in_=ones_b[:, :], compare_op=ALU.is_gt, fill=0.0,
                                    base=0, pattern=[[1, P]], channel_multiplier=-1))
            make(pool.affine_select(out=earlier[:, :, :], in_=earlier[:, :, :], compare_op=ALU.is_gt, fill=0.0,
                                    base=0, pattern=[[1, E], [-1, E]], channel_multiplier=0))
            assert made.now() == NCONST

            def window_order(n):
                if not (isinstance(n, int) and n == 0):
                    pool.wait_ge(xt_ps, n)
                src = by_window(x_sb[:, bass.ds(n, 1), :])
                dst = xw[:, :].rearrange("c (s w h k) -> c s w h k", w=W // WS, h=WS, k=WS)
                for s in range(2):
                    pool.tensor_copy(dst[:, s, :, :, :], src[:, s, :, :, :]).then_inc(x_win, 1)

            def gather_round(g, r, opening=False):
                n = g * ROUNDS + r
                if not opening:
                    for u in range(RING):
                        pool.wait_ge(xg_in[u], n * 16)
                pool.tensor_copy(gidx[:, :], src_i[:, bass.ts(r, RING)]).then_inc(gidx_ok, 1)
                for u in range(RING):
                    free = [] if opening else [(xgt_ps, (n - 1) * RING + u + 1)]
                    wait_apart(pool, (gidx_ok, n + 1), *free)
                    pool.indirect_dma_start(
                        out=xg[:, u, :], out_offset=None, in_=tn_dram[g],
                        in_offset=bass.IndirectOffsetOnAxis(ap=gidx[:, u:u + 1], axis=0)).then_inc(xg_in[u], 16)

            def gather_back(g, i, opening=False):
                n = g * NCH + i
                if not opening:
                    for j in range(TPC):
                        pool.wait_ge(yg_in[j], n * 32)
                pool.tensor_copy(cidx[:, :, :], slot_i[:, g, :, bass.ts(i, TPC)]).then_inc(cidx_ok, 1)
                wait_apart(pool, (cidx_ok, n + 1), *([] if opening else [(o_ok, n)]))
                for j in range(TPC):
                    for k in range(2):
                        pool.indirect_dma_start(
                            out=yg[:, k, j, :], out_offset=None, in_=y_dram[g],
                            in_offset=bass.IndirectOffsetOnAxis(ap=cidx[:, k, j:j + 1], axis=0)
                        ).then_inc(yg_in[j], 16)

            for g in range(GROUPS):
                if g == 0:
                    for n in range(SPB):
                        pool.wait_ge(x_in[min(n, 1)], 16)
                        window_order(n)
                    pool.wait_ge(x_in[2], 16)
                    looped(pool, SPB, NCH, window_order)
                else:
                    pool.wait_ge(x_in[g + 2], 16)
                    window_order(g * NCH)
                    pool.wait_ge(y_out, g * ROUNDS * 16)

                    def back_step(i):
                        gather_back(g - 1, i, opening=(g == 1 and isinstance(i, int)))
                        window_order(g * NCH + i + 1)
                    back_step(0)
                    looped(pool, 1, NCH - 1, back_step)
                    gather_back(g - 1, NCH - 1)
                pool.wait_ge(src_ok, g + 1)
                pool.wait_ge(tn_out, (g + 1) * NCH * 16)
                gather_round(g, 0, opening=(g == 0))
                looped(pool, 1, ROUNDS, lambda r: gather_round(g, r))
            pool.wait_ge(y_out, GROUPS * ROUNDS * 16)
            looped(pool, 0, NCH, lambda i: gather_back(GROUPS - 1, i))

        @block.tensor
        def _(pe):
            def transposes(dst, srcs, done):
                for j, s in enumerate(srcs):
                    mm = pe.transpose(dst[:, j * P:(j + 1) * P], s, ident[:, :])
                mm.then_inc(done, 1)

            pe.wait_ge(pool_c, NCONST)
            pe.wait_ge(w_in, 9 * 16)
            transposes(Q, [raw[:, n, :] for n in range(3)], wt_ps)
            pe.wait_ge(wt_sb, 2)
            pe.matmul(K[:, 0:P], raw[:, 3, :], woT[:, :], start=True, stop=True)
            pe.matmul(K[:, P:2 * P], bv_b[:, :], woT[:, :], start=True, stop=False)
            pe.matmul(K[:, P:2 * P], ones_row[:, :], bo_row[:, :], start=False, stop=True).then_inc(wvo_ps, 1)
            pe.wait_ge(wvo_sb, 4)

            def x_tiles(n):
                return [xw[:, j * P:(j + 1) * P] for j in range(TPC)]

            def step(g):
                def run(i, n, new, mid, old, back):
                    if new:
                        if not (isinstance(n, int) and n == 0):
                            pe.wait_ge(xb_ok, n)
                            pe.wait_ge(xn_ok, n)
                        if g > 0 and not (isinstance(i, int) and i <= 1):
                            pe.wait_ge(ot_ok, (g - 1) * NCH + i - 1)
                        pe.wait_ge(x_win, 2 * n + 2)
                        transposes(XT, x_tiles(n), xt_ps)
                    if mid:
                        pe.wait_ge(qkv_ok, n * 3 - 1)
                        if not (isinstance(n, int) and n == 1):
                            pe.wait_ge(sc_ok, n - 1)
                        for j in range(TPC):
                            t = slice(j * P, (j + 1) * P)
                            mm = pe.matmul(S[:, t], q_sb[:, t], k_sb[:, t], start=True, stop=True)
                        mm.then_inc(s_ps, 1)
                    if old:
                        pe.wait_ge(tn_ok, n - 1)
                        transposes(TNT, [tn_sb[:, j, :] for j in range(TPC)], tnt_ps)
                    if new:
                        pe.wait_ge(xn_ok, n + 1)
                        if not (isinstance(n, int) and n < 3):
                            pe.wait_ge(rk_ok, n - 2)
                            pe.wait_ge(lg_ok, n - 2)
                        if not (isinstance(n, int) and n < 2):
                            pe.wait_ge(t_ok, n - 1)
                        transposes(XNT, [xn[:, j, :] for j in range(TPC)], xnt_ps)
                    if mid:
                        pe.wait_ge(p_ok, n)
                        if old:
                            pe.wait_ge(tnt_ok, n - 1)
                        transposes(PT, [prob[:, j, :] for j in range(TPC)], pt_ps)
                    if old:
                        pe.wait_ge(tnt_ok, n - 1)
                        if new:
                            pe.wait_ge(xnt_ok, n + 1)
                        else:
                            pe.wait_ge(rk_ok, n - 2)
                        for j in range(TPC):
                            mm = pe.matmul(LG[:, j * E:(j + 1) * E], tnT[:, j * P:(j + 1) * P], wg_sb[:, :],
                                           start=True, stop=True)
                        mm.then_inc(lg_ps, 1)
                    if new:
                        pe.wait_ge(xnt_ok, n + 1)
                        if not (isinstance(n, int) and n == 0):
                            pe.wait_ge(qkv_ok, n * 3)
                        pe.matmul(Q[:, :], wqT[:, :], xnT[:, :], start=True, stop=True)
                        pe.matmul(K[:, :], wkT[:, :], xnT[:, :], start=True, stop=True)
                        for j in range(TPC):
                            t = slice(j * P, (j + 1) * P)
                            mm = pe.matmul(VO[:, t], xnT[:, t], wvo[:, :], start=True, stop=True)
                        mm.then_inc(qkv_ps, 1)
                    if mid:
                        pe.wait_ge(pt_ok, n)
                        if not (isinstance(n, int) and n == 1):
                            pe.wait_ge(t_ok, n - 1)
                        pe.wait_ge(qkv_ok, n * 3)
                        if old:
                            pe.wait_ge(lg_ok, n - 1)
                        for j in range(TPC):
                            t = slice(j * P, (j + 1) * P)
                            pe.matmul(Y[:, t], pT[:, t], vo_sb[:, j, :], start=True, stop=True)
                            mm = pe.matmul(DN[:, j:j + 1], pT[:, t], ones_f[:, 0:1], start=True, stop=True)
                        mm.then_inc(y_ps, 1)
                    if old:
                        pe.wait_ge(both_ok, n - 1)
                        if mid:
                            pe.wait_ge(den_ok, n)
                        own = both[:, bass.ds((n - 2 - g * NCH) * TPC, TPC), :].rearrange("p j e -> p (j e)")
                        old_ = cum[:, bass.ds((n - 2 - g * NCH) * TPC, TPC), :].rearrange("p j e -> p (j e)")
                        pe.matmul(RK, before_b[:, :], own, start=True, stop=False)
                        pe.matmul(RK, ones_b[:, :], old_, start=False, stop=True).then_inc(rk_ps, 1)
                    if back:
                        pe.wait_ge(xb_ok, n + 1 if new else n)
                        back_turn(n - 1 - NCH)
                return run

            def back_turn(n):
                pe.wait_ge(o_ok, n + 1)
                transposes(OT, [o2[:, j, :] for j in range(TPC)], ot_ps)

            def expert_round(g, r, start=False, end=False):
                n0 = (g * ROUNDS + r) * RING

                def turn_x(u):
                    n = n0 + u
                    pe.wait_ge(xg_in[u % RING], (g * ROUNDS + r + u // RING + 1) * 16)
                    if not (start and u < 2 and g == 0):
                        pe.wait_ge(xgt_ok, n - 1)
                    pe.transpose(bank[u % 2][:, 0:P], xg[:, u % RING, :], ident[:, :]).then_inc(xgt_ps, 1)

                def hidden(u):
                    n = n0 + u
                    pe.wait_ge(xgt_ok, n + 1)
                    if not (start and u < 2 and g == 0):
                        pe.wait_ge(hid_ok, n - 1)
                    at = pe.value_load(exp_01[0:1, bass.ds(r * RING + u, 1)], min_val=0, max_val=(E - 1) * 2 * M)
                    w = w01[:, :, :, :].rearrange("p e a m -> p (e a m)")
                    pe.matmul(bank[2 + u % 2][:, :], xgT[:, u % 2, :], w[:, bass.ds(at, 2 * M)],
                              start=True, stop=True).then_inc(h_ps, 1)

                def turn_h(u):
                    n = n0 + u
                    pe.wait_ge(hid_ok, n + 1)
                    if not (start and u < 2 and g == 0):
                        pe.wait_ge(ht_ok, n - 1)
                    pe.transpose(bank[4 + u % 2][:, 0:P], hid[:, u % 2, 0:P], ident[:, :])
                    pe.transpose(bank[4 + u % 2][:, P:M], hid[:, u % 2, P:M], ident[:, :]).then_inc(ht_ps, 1)

                def down(u):
                    n = n0 + u
                    pe.wait_ge(ht_ok, n + 1)
                    if not (start and u < 2 and g == 0):
                        pe.wait_ge(ye_ok, n - 1)
                    at = pe.value_load(exp_2[0:1, bass.ds(r * RING + u, 1)], min_val=0, max_val=(E - 1) * 2 * D)
                    w = w2_sb[:, :, :, :].rearrange("p e k d -> p (e k d)")
                    pe.matmul(bank[6 + u % 2][:, 0:D], hT[:, u % 2, 0:P], w[:, bass.ds(at, D)],
                              start=True, stop=False)
                    pe.matmul(bank[6 + u % 2][:, 0:D], hT[:, u % 2, P:M], w[:, bass.ds(at + D, D)],
                              start=False, stop=True).then_inc(ye_ps, 1)

                if start:
                    turn_x(0)
                for u in range(RING):
                    if not (end and u == RING - 1):
                        turn_x(u + 1)
                    hidden(u)
                    if not (start and u < 2):
                        down(u - 2)
                    if not (start and u < 1):
                        turn_h(u - 1)
                if end:
                    down(RING - 2)
                    turn_h(RING - 1)
                    down(RING - 1)

            for g in range(GROUPS):
                conv_steps(pe, g, step(g))
                pe.wait_ge(rk_ok, (g + 1) * NCH)
                pe.matmul(XNT[:, 0:E], ones_b[:, :], cum[:, NT, :], start=True, stop=True).then_inc(tot_ps, 1)

                def pick(i, first=False, last=False):
                    for k in range(2):
                        n = (g * NT + i) * 2 + k
                        pe.wait_ge(sel_ok, n + 1)
                        pe.matmul(Q[:, 0:2 * TILES], sel_p[:, k, :],
                                  sel_t[:, k, :, :].rearrange("p a t -> p (a t)"),
                                  start=(first and k == 0), stop=(last and k == 1),
                                  ).then_inc(sel_used, 1)
                pe.wait_ge(qkv_ok, (g + 1) * NCH * 3)
                pick(0, first=True)
                looped(pe, 1, NT - 1, pick)
                pick(NT - 1, last=True)
                pe.wait_ge(src_ok, g + 1)
                if g == 0:
                    pe.wait_ge(e_in, 3 * 16)
                pe.wait_ge(exp_ok, g + 1)
                if g > 0:
                    pe.wait_ge(ot_ok, g * NCH)
                expert_round(g, 0, start=True)
                looped(pe, 1, ROUNDS - 1, lambda r: expert_round(g, r))
                expert_round(g, ROUNDS - 1, end=True)
                pe.wait_ge(ye_ok, (g + 1) * TILES)

            def last_turn(n):
                pe.wait_ge(ot_ok, n)
                back_turn(n)
            looped(pe, (GROUPS - 1) * NCH, GROUPS * NCH, last_turn)

        @block.scalar
        def _(act):
            def out_copy(n):
                act.wait_ge(ot_ps, n + 1)
                v = by_window(x_sb[:, bass.ds(n, 1), :])
                src = OT[:, :].rearrange("c (s w h k) -> c s w h k", s=CHUNK // W // WS, h=WS, k=WS)
                for s in range(2):
                    ins = act.copy(v[:, s, :, :, :], src[:, s, :, :, :])
                    if s == 0:
                        ins.then_inc(ot_half, 1)
                ins.then_inc(ot_ok, 1)

            def step(g):
                def run(i, n, new, mid, old, back):
                    if mid:
                        act.wait_ge(sc_ok, n)
                        if not (isinstance(n, int) and n == 1):
                            act.wait_ge(pt_ps, n - 1)
                        h = P // 2
                        act.activation(prob[0:h, :, 0:h], sc[0:h, :, :], ACT.Exp, scale=SCALE)
                        act.activation(prob[h:P, :, h:P], sc[h:P, :, :], ACT.Exp, scale=SCALE).then_inc(p_ok, 1)
                    if new:
                        act.wait_ge(stats, n + 1)
                        act.wait_ge(xb_ok, n + 1)
                        if not (isinstance(n, int) and n == 0):
                            act.wait_ge(xnt_ps, n)
                        for j in range(TPC):
                            ins = act.activation(xn[:, j, :], XT[:, j * P:(j + 1) * P], ACT.Identity,
                                                 bias=nb[:, j:j + 1], scale=rs[:, j:j + 1])
                        ins.then_inc(xn_ok, 1)
                    if old:
                        act.wait_ge(tnt_ps, n - 1)
                        if not (isinstance(n, int) and n == 2):
                            act.wait_ge(lg_ps, n - 2)
                        act.copy(tnT[:, :], TNT[:, :]).then_inc(tnt_ok, 1)
                    if new:
                        act.wait_ge(xnt_ps, n + 1)
                        if not (isinstance(n, int) and n == 0):
                            act.wait_ge(qkv_ps, n)
                        act.copy(xnT[:, :], XNT[:, :]).then_inc(xnt_ok, 1)
                    if mid:
                        act.wait_ge(pt_ps, n)
                        if not (isinstance(n, int) and n == 1):
                            act.wait_ge(y_ps, n - 1)
                        act.copy(pT[:, :], PT[:, :]).then_inc(pt_ok, 1)
                    if new:
                        act.wait_ge(qkv_ps, n + 1)
                        if not (isinstance(n, int) and n == 0):
                            act.wait_ge(s_ps, n)
                        act.activation(q_sb[:, :], Q[:, :], ACT.Identity, bias=bcols[:, 0:1]).then_inc(qkv_ok, 1)
                        act.activation(k_sb[:, :], K[:, :], ACT.Identity, bias=bcols[:, 1:2]).then_inc(qkv_ok, 1)
                        if not (isinstance(n, int) and n == 0):
                            act.wait_ge(y_ps, n)
                        act.copy(vo_sb[:, :, :], by_tile(VO)).then_inc(qkv_ok, 1)
                    if old:
                        act.wait_ge(dm_ok, n - 1)
                        act.activation(ex[:, :, :], dm[:, :, :], ACT.Exp).then_inc(ex_ok, 1)
                    if back:
                        out_copy(n - 1 - NCH)
                return run

            def expert_round(g, r, start=False):
                n0 = (g * ROUNDS + r) * RING
                if start:
                    x_copy(g, n0, 0, True)
                for u in range(RING):
                    x_copy(g, n0, u + 1, start)
                    silu(g, n0, u, start)

            def x_copy(g, n0, u, start):
                n = n0 + u
                act.wait_ge(xgt_ps, n + 1)
                if not (start and u < 2 and g == 0):
                    act.wait_ge(h_ps, n - 1)
                act.copy(xgT[:, u % 2, :], bank[u % 2][:, 0:P]).then_inc(xgt_ok, 1)

            def silu(g, n0, u, start):
                n = n0 + u
                act.wait_ge(h_ps, n + 1)
                if not (start and u < 2 and g == 0):
                    act.wait_ge(hid_ok, n - 1)
                act.activation(sil[:, u % 2, :], bank[2 + u % 2][:, 0:M], ACT.Silu).then_inc(sil_ok, 1)

            for g in range(GROUPS):
                conv_steps(act, g, step(g))
                expert_round(g, 0, start=True)
                looped(act, 1, ROUNDS - 1, lambda r: expert_round(g, r))
                n0 = (g * ROUNDS + ROUNDS - 1) * RING
                for u in range(RING):
                    if u < RING - 1:
                        x_copy(g, n0, u + 1, False)
                    silu(g, n0, u, False)
            looped(act, (GROUPS - 1) * NCH, GROUPS * NCH, out_copy)

        @block.vector
        def _(dve):
            tick = Ticks()

            def then(ins):
                ins.then_inc(vec, 1)
                tick.up()

            def settled():
                dve.wait_ge(vec, tick.now())

            def spread(a, n):
                return a.unsqueeze(2).to_broadcast([P, TPC, n])

            dve.wait_ge(pool_c, NCONST)
            then(dve.memset(prob[:, :, :], 0.0))
            then(dve.memset(cum[:, 0, :], 0.0))
            dve.wait_ge(w_in, 9 * 16)
            dve.tensor_copy(bv_b[:, :], bcols[:, 2:3].to_broadcast([P, P])).then_inc(wt_sb, 1)
            dve.wait_ge(wt_ps, 1)
            dve.tensor_copy(woT[:, :], Q[:, 2 * P:3 * P]).then_inc(wt_sb, 1)
            dve.tensor_copy(wqT[:, :], Q[:, 0:P]).then_inc(wvo_sb, 1)
            dve.tensor_copy(wkT[:, :], Q[:, P:2 * P]).then_inc(wvo_sb, 1)
            dve.wait_ge(wvo_ps, 1)
            dve.tensor_copy(wvo[:, :], K[:, 0:P]).then_inc(wvo_sb, 1)
            dve.tensor_copy(bvo[:, :], K[:, P:2 * P]).then_inc(wvo_sb, 1)
            dve.wait_ge(wvo_sb, 4)

            def norm_stats(rows, st_, mv_, rs_, eps, beside=None):
                for j in range(TPC):
                    then(dve.bn_stats(st_[:, j, :], rows[j]))
                if beside:
                    beside()
                wait_apart(dve, (vec, tick.now()))
                for j in range(TPC):
                    then(dve.bn_aggr(mv_[:, j, :], st_[:, j, :]))
                settled()
                then(dve.tensor_scalar(var[:, :], mv_[:, :, 1], eps, None, ALU.add)); settled()
                then(dve.tensor_scalar(bits[:, :], var[:, :].bitcast(I32), 1, None, ALU.logical_shift_right)); settled()
                then(dve.tensor_scalar(rs_[:, :].bitcast(I32), bits[:, :], -1.0, float(0x5f3759df),
                                       ALU.mult, ALU.add)); settled()
                for _ in range(3):
                    then(dve.tensor_tensor(sq[:, :], rs_[:, :], rs_[:, :], ALU.mult)); settled()
                    then(dve.scalar_tensor_tensor(out=sq[:, :], in0=sq[:, :], scalar=-0.5, in1=var[:, :],
                                                  op0=ALU.mult, op1=ALU.mult)); settled()
                    then(dve.scalar_tensor_tensor(out=rs_[:, :], in0=sq[:, :], scalar=1.5, in1=rs_[:, :],
                                                  op0=ALU.add, op1=ALU.mult)); settled()

            def combine(n):
                for j in range(TPC):
                    dve.wait_ge(yg_in[j], (n + 1) * 32)
                    tt = t_sb[:, bass.ds(n * TPC + j, 1), :].rearrange("p a d -> p (a d)")
                    then(dve.scalar_tensor_tensor(out=o1[:, j, :], in0=yg[:, 0, j, :],
                                                  scalar=gate[:, 0, bass.ds(n * TPC + j, 1)],
                                                  in1=tt, op0=ALU.mult, op1=ALU.add))
                settled()
                if not (isinstance(n, int) and n == 0):
                    dve.wait_ge(ot_ps, n)
                for j in range(TPC):
                    ins = dve.scalar_tensor_tensor(out=o2[:, j, :], in0=yg[:, 1, j, :],
                                                   scalar=gate[:, 1, bass.ds(n * TPC + j, 1)],
                                                   in1=o1[:, j, :], op0=ALU.mult, op1=ALU.add)
                    if j < TPC - 1:
                        then(ins)
                ins.then_inc(o_ok, 1)
                dve.wait_ge(o_ok, n + 1)

            def step(g):
                def run(i, n, new, mid, old, back):
                    if new:
                        dve.wait_ge(xt_ps, n + 1)
                        if not (isinstance(n, int) and n == 0):
                            dve.wait_ge(xn_ok, n)
                        def with_bias():
                            dve.tensor_tensor(t_rows(n), by_tile(XT), bvo[:, :].unsqueeze(1).to_broadcast([P, TPC, P]),
                                              ALU.add).then_inc(xb_ok, 1)
                        norm_stats([XT[:, j * P:(j + 1) * P] for j in range(TPC)], st, mv, rs, LN_C_EPS, with_bias)
                        dve.scalar_tensor_tensor(out=nb[:, :], in0=mv[:, :, 0], scalar=-1.0, in1=rs[:, :],
                                                 op0=ALU.mult, op1=ALU.mult).then_inc(stats, 1)
                    if mid:
                        dve.wait_ge(s_ps, n)
                        h = P // 2
                        sv = by_tile(S)
                        then(dve.tensor_reduce(smax[0:h, :], sv[0:h, :, 0:h], AX.X, ALU.max))
                        then(dve.tensor_reduce(smax[h:P, :], sv[h:P, :, h:P], AX.X, ALU.max))
                        settled()
                        if not (isinstance(n, int) and n == 1):
                            dve.wait_ge(p_ok, n - 1)
                        then(dve.tensor_tensor(sc[0:h, :, :], sv[0:h, :, 0:h],
                                               smax[0:h, :].unsqueeze(2).to_broadcast([h, TPC, h]), ALU.subtract))
                        dve.tensor_tensor(sc[h:P, :, :], sv[h:P, :, h:P],
                                          smax[h:P, :].unsqueeze(2).to_broadcast([h, TPC, h]),
                                          ALU.subtract).then_inc(sc_ok, 1)
                    if old:
                        top2(g, n - 2)
                    if mid:
                        dve.wait_ge(y_ps, n)
                        dve.reciprocal(den[:, :], DN).then_inc(den_ok, 1)
                        dve.wait_ge(den_ok, n)
                        dve.wait_ge(xb_ok, n)
                        m = n - 1
                        rows = [t_sb[:, bass.ds(m * TPC + j, 1), :].rearrange("p a d -> p (a d)") for j in range(TPC)]
                        for j in range(TPC):
                            ins = dve.scalar_tensor_tensor(out=rows[j], in0=Y[:, j * P:(j + 1) * P],
                                                           scalar=den[:, j:j + 1], in1=rows[j],
                                                           op0=ALU.mult, op1=ALU.add)
                            if j < TPC - 1:
                                then(ins)
                        ins.then_inc(t_ok, 1)
                        wait_apart(dve, (t_ok, n), (vec, tick.now()))
                        norm_stats(rows, st2, mv2, rs2, LN_T_EPS)
                        if not (isinstance(m, int) and m == 0):
                            dve.wait_ge(tnt_ps, m)
                            dve.wait_ge(tn_out, m * 16)
                        for j in range(TPC):
                            ins = dve.tensor_scalar(tn_sb[:, j, :],
                                                    rows[j], mv2[:, j, 0:1], rs2[:, j:j + 1],
                                                    ALU.subtract, ALU.mult)
                            if j < TPC - 1:
                                then(ins)
                        settled()
                        ins.then_inc(tn_ok, 1)
                    if old:
                        dve.wait_ge(rk_ps, n - 1)
                        dve.tensor_copy(rank[:, bass.ds((n - 2 - g * NCH) * TPC, TPC), :].rearrange("p j e -> p (j e)"),
                                        RK).then_inc(rk_ok, 1)
                        weights(n - 2)
                    if back:
                        combine(n - 1 - NCH)
                return run

            def t_rows(n):
                return t_sb[:, bass.ds(n * TPC, TPC), :]

            def top2(g, n):
                dve.wait_ge(lg_ps, n + 1)
                lv = LG.rearrange("p (j e) -> p j e", j=TPC)
                tiles = bass.ds(n * TPC, TPC)
                dve.tensor_copy(lg[:, :, :], lv).then_inc(lg_ok, 1)
                dve.wait_ge(lg_ok, n + 1)
                for k, (v, top) in enumerate(((lg, m1), (lg2, m2))):
                    then(dve.tensor_reduce(top[:, :], v[:, :, :], AX.X, ALU.max)); settled()
                    then(dve.tensor_tensor(eq[:, :, :], v[:, :, :], spread(top[:, :], E), ALU.is_equal)); settled()
                    then(dve.tensor_tensor(eq[:, :, :], eq[:, :, :], rev_e[:, :, :], ALU.mult)); settled()
                    then(dve.tensor_reduce(pick[:, :], eq[:, :, :], AX.X, ALU.max)); settled()
                    then(dve.tensor_tensor(oh[:, k, tiles, :], rev_e[:, :, :], spread(pick[:, :], E),
                                           ALU.is_equal)); settled()
                    if k == 0:
                        then(dve.scalar_tensor_tensor(out=lg2[:, :, :], in0=oh[:, 0, tiles, :], scalar=LOWEST,
                                                      in1=lg[:, :, :], op0=ALU.mult, op1=ALU.add)); settled()
                if not (isinstance(n, int) and n == 0):
                    dve.wait_ge(ex_ok, n)
                then(dve.tensor_tensor(dm[:, 0, :], m2[:, :], m1[:, :], ALU.subtract)); settled()
                dve.memset(dm[:, 1, :], 0.0).then_inc(dm_ok, 1)
                own = bass.ds((n - g * NCH) * TPC, TPC)
                then(dve.tensor_tensor(both[:, own, :], oh[:, 0, tiles, :], oh[:, 1, tiles, :], ALU.add)); settled()
                for j in range(TPC):
                    c0 = bass.ds((n - g * NCH) * TPC + j, 1)
                    c1 = bass.ds((n - g * NCH) * TPC + j + 1, 1)
                    ins = dve.tensor_tensor(cum[:, c1, :], cum[:, c0, :], both[:, c0, :], ALU.add)
                    if j < TPC - 1:
                        then(ins); settled()
                ins.then_inc(both_ok, 1)

            def weights(n):
                tiles = bass.ds(n * TPC, TPC)
                dve.wait_ge(both_ok, n + 1)
                dve.wait_ge(ex_ok, n + 1)
                then(dve.tensor_scalar(ex[:, 1, :], ex[:, 0, :], 1.0, None, ALU.add)); settled()
                then(dve.reciprocal(gate[:, 0, tiles], ex[:, 1, :])); settled()
                then(dve.tensor_tensor(gate[:, 1, tiles], gate[:, 0, tiles], ex[:, 0, :], ALU.mult))

            def route(g):
                dve.wait_ge(tot_ps, g + 1)
                then(dve.tensor_scalar(tot_i[:, :], XNT[:, 0:E], float(P - 1), None, ALU.add)); settled()
                then(dve.tensor_scalar(cnt_i[:, :], tot_i[:, :], 7, None, ALU.logical_shift_right)); settled()
                then(dve.tensor_copy(ntile[:, :], cnt_i[:, :])); settled()
                then(dve.tensor_tensor(prod[:, :, :], earlier[:, :, :],
                                       ntile[:, :].unsqueeze(1).to_broadcast([P, E, E]), ALU.mult)); settled()
                then(dve.tensor_reduce(first[:, :], prod[:, :, :], AX.X, ALU.add)); settled()
                then(dve.tensor_tensor(ends[:, :], first[:, :], ntile[:, :], ALU.add))
                then(dve.tensor_scalar(base[:, :], first[:, :], float(P), None, ALU.mult)); settled()
                then(dve.tensor_tensor(place[:, :, :], rank[:, :, :],
                                       base[:, :].unsqueeze(1).to_broadcast([P, NT, E]), ALU.add)); settled()
                for k in range(2):
                    then(dve.tensor_tensor(pp[:, :, :], place[:, :, :], oh[:, k, g * NT:(g + 1) * NT, :],
                                           ALU.mult)); settled()
                    then(dve.tensor_reduce(slot[:, k, :], pp[:, :, :], AX.X, ALU.add)); settled()
                then(dve.tensor_copy(slot_i[:, g, :, :], slot[:, :, :])); settled()
                then(dve.tensor_scalar(hi_i[:, :, :], slot_i[:, g, :, :], 7, None, ALU.logical_shift_right))
                then(dve.tensor_scalar(lo_i[:, :, :], slot_i[:, g, :, :], P - 1, None, ALU.bitwise_and)); settled()
                then(dve.tensor_copy(hi_f[:, :, :], hi_i[:, :, :]))
                then(dve.tensor_copy(lo_f[:, :, :], lo_i[:, :, :])); settled()

                def pick_rows(i):
                    for k in range(2):
                        n = (g * NT + i) * 2 + k
                        if not (isinstance(i, int) and i == 0 and g == 0):
                            dve.wait_ge(sel_used, n - 1)
                        col = bass.ds(i, 1)
                        then(dve.tensor_scalar(sel_p[:, k, :], iota_p[:, :], lo_f[:, k, col], None, ALU.is_equal))
                        then(dve.tensor_scalar(sel_t[:, k, 0, :], iota_t[:, :], hi_f[:, k, col], tile_row[:, col],
                                               ALU.is_equal, ALU.mult))
                        settled()
                        dve.tensor_scalar(sel_t[:, k, 1, :], iota_t[:, :], hi_f[:, k, col], part_col[:, 0:1],
                                          ALU.is_equal, ALU.mult).then_inc(sel_ok, 1)
                pick_rows(0)
                looped(dve, 1, NT, pick_rows, tick)
                then(dve.tensor_tensor(done[:, :, :], iota_te[:, :, :],
                                       ends[:, :].unsqueeze(1).to_broadcast([P, TILES, E]), ALU.is_ge)); settled()
                then(dve.tensor_reduce(exp_f[:, :], done[:, :, :], AX.X, ALU.add)); settled()
                then(dve.tensor_scalar(exp_f[:, :], exp_f[:, :], float(E - 1), None, ALU.min)); settled()
                then(dve.tensor_scalar(exp_01[:, :], exp_f[:, :], float(2 * M), None, ALU.mult)); settled()
                dve.tensor_scalar(exp_2[:, :], exp_f[:, :], float(2 * D), None, ALU.mult).then_inc(exp_ok, 1)
                dve.wait_ge(sel_used, (g + 1) * NT * 2)
                then(dve.tensor_copy(lows[:, :], Q[:, TILES:2 * TILES])); settled()
                then(dve.scalar_tensor_tensor(out=src_f[:, :], in0=Q[:, 0:TILES], scalar=float(P), in1=lows[:, :],
                                              op0=ALU.mult, op1=ALU.add)); settled()
                dve.tensor_copy(src_i[:, :], src_f[:, :]).then_inc(src_ok, 1)

            def product(g, n0, u, start):
                n = n0 + u
                dve.wait_ge(sil_ok, n + 1)
                if not (start and u < 2 and g == 0):
                    dve.wait_ge(ht_ps, n - 1)
                dve.tensor_tensor(hid[:, u % 2, :], sil[:, u % 2, :], bank[2 + u % 2][:, M:2 * M],
                                  ALU.mult).then_inc(hid_ok, 1)

            def ht_copy(g, n0, u, start):
                n = n0 + u
                dve.wait_ge(ht_ps, n + 1)
                if not (start and u < 2 and g == 0):
                    dve.wait_ge(ye_ps, n - 1)
                dve.tensor_copy(hT[:, u % 2, :], bank[4 + u % 2][:, 0:M]).then_inc(ht_ok, 1)

            def experts(g):
                def step(n0, r2, u, start=False, end=0):
                    if end < 1:
                        product(g, n0, u, start)
                    if not (start and u < 2):
                        v = u - 2
                        m = n0 + v
                        dve.wait_ge(ye_ps, m + 1)
                        if v % RING == 0 and not (g == 0 and start):
                            dve.wait_ge(y_out, ((m_round(n0, v)) - 1) * 16)
                        dve.tensor_copy(ys[:, (v // RING) % 2, v % RING, :], bank[6 + v % 2][:, 0:D]).then_inc(ye_ok, 1)
                    if end < 2 and not (start and u < 1):
                        ht_copy(g, n0, u - 1, start)

                def m_round(n0, v):
                    return round_of[0] + v // RING
                round_of = [None]

                def two_rounds(r2, start=False):
                    n0 = (g * ROUNDS + r2 * 2) * RING
                    round_of[0] = g * ROUNDS + r2 * 2
                    for u in range(2 * RING):
                        step(n0, r2, u, start)
                two_rounds(0, start=True)
                looped(dve, 1, ROUNDS // 2, two_rounds)
                n0 = (g + 1) * ROUNDS * RING
                round_of[0] = (g + 1) * ROUNDS
                step(n0, None, 0, end=1)
                step(n0, None, 1, end=2)

            for g in range(GROUPS):
                conv_steps(dve, g, step(g), tick)
                route(g)
                experts(g)
            looped(dve, (GROUPS - 1) * NCH, GROUPS * NCH, combine, tick)


_INS = ["x", "L0_conv_wq", "L0_conv_bq", "L0_conv_wk", "L0_conv_bk", "L0_conv_wv", "L0_conv_bv",
        "L0_conv_wo", "L0_conv_bo", "L0_ffn_wg", "L0_ffn_w0", "L0_ffn_w1", "L0_ffn_wo"]


def kernel(**inputs):
    import numpy as _np
    import concourse.bacc as _bacc
    from concourse import mybir as _mybir
    from concourse.bass_utils import run_bass_kernel_spmd as _run

    nc = _bacc.Bacc("TRN2", target_bir_lowering=False, num_devices=1)
    arrays, args = {}, []
    for name in _INS:
        a = _np.ascontiguousarray(inputs[name])
        arrays[f"in_{name}"] = a
        args.append(nc.dram_tensor(f"in_{name}", a.shape, _mybir.dt.from_np(a.dtype), kind="ExternalInput").ap())
    shape = inputs["x"].shape
    out = nc.dram_tensor("out_0", shape, _mybir.dt.from_np(_np.dtype("float32")), kind="ExternalOutput").ap()
    emit(nc, *args, out)
    r = _run(nc, [arrays], core_ids=[0])
    return r.results[0]["out_0"]
```

```python
from contextlib import ExitStack

import concourse.bass as bass
from concourse import mybir

F32 = mybir.dt.float32
BF16 = mybir.dt.bfloat16
F16 = mybir.dt.float16
I32 = mybir.dt.int32
U32 = mybir.dt.uint32
ALU = mybir.AluOpType
ACT = mybir.ActivationFunctionType
AX = mybir.AxisListType

P = 128
WS = 8
TPC = 4
CHUNK = TPC * P
RING = 8
HALF = RING // 2
LAG = 3


class Ticks:

    def __init__(self):
        self.base, self.count = 0, 0

    def up(self, n=1):
        self.count += n
        return self.base + self.count

    def now(self):
        return self.base + self.count


def emit(nc, x, wq, bq, wk, bk, wv, bv, wo, bo, wg, w0, w1, w2, out):
    B, C, H, W = x.shape
    E, D, M = w0.shape
    assert C == P and D == P and M == 2 * P and H * W % CHUNK == 0
    GROUPS = 2
    NCH = B * H * W // CHUNK // GROUPS
    NT = NCH * TPC
    PAIRS = 2 * NT * P
    TILES = -(-(PAIRS // P + E - 1) // RING) * RING
    ROUNDS = TILES // RING
    MID = NT * P // 2
    assert MID <= 2048
    STEPS = NCH + LAG
    SPB = H * W // CHUNK
    SCALE = float(C) ** -0.5
    LN_C_EPS, LN_T_EPS = 1e-6, 1e-5

    tn_dram = [nc.dram_tensor(f"normed_{g}", (NT * P, D), F32, kind="Internal").ap() for g in range(GROUPS)]
    y_dram = [nc.dram_tensor(f"expert_rows_{g}", (TILES * P, D), F32, kind="Internal").ap() for g in range(GROUPS)]

    with ExitStack() as ctx:
        def sb(name, shape, dt=F32):
            return ctx.enter_context(nc.sbuf_tensor(name, shape, dt))

        def sem(name):
            return ctx.enter_context(nc.semaphore(name))

        ident = sb("ident", [P, P])
        ones_row = sb("ones_row", [1, P])
        ones_f = sb("ones_f", [P, P])
        ones_b = sb("ones_b", [P, P], BF16)
        before_b = sb("before_b", [P, P], BF16)
        earlier = sb("earlier", [P, E, E])
        inside = sb("inside", [P, E, NT], BF16)
        iota_e = sb("iota_e", [P, E])
        token_id = sb("token_id", [P, NT])
        iota_p = sb("iota_p", [P, P], F16)
        iota_t = sb("iota_t", [P, TILES], F16)
        iota_te = sb("iota_te", [P, TILES, E], BF16)
        eps = sb("eps", [P, 2, TPC])
        raw = sb("raw", [P, 4, P])
        wqT = sb("wqT", [P, P])
        wkT = sb("wkT", [P, P])
        woT = sb("woT", [P, P])
        wvo = sb("wvo", [P, P])
        bcols = sb("bcols", [P, 3])
        bo_row = sb("bo_row", [1, P])
        bv_b = sb("bv_b", [P, P])
        bvo = sb("bvo", [P, P])
        wg_sb = sb("wg_sb", [P, E])
        w01 = sb("w01", [P, E, 2, M])
        w2_sb = sb("w2_sb", [P, E, 2, D])

        x_sb = sb("x_sb", [P, GROUPS * NCH, CHUNK])
        t_sb = sb("t_sb", [P, GROUPS * NT, D])
        top_v = sb("top_v", [P, NT, 2])
        top_e = sb("top_e", [P, NT, 2])
        gate = sb("gate", [P, 2, GROUPS * NT])

        xw = sb("xw", [P, CHUNK])
        st = sb("st", [P, TPC, 6])
        mv = sb("mv", [P, 2, TPC, 2])
        var = sb("var", [P, 2, TPC])
        bits = sb("bits", [P, 2, TPC], I32)
        sq = sb("sq", [P, 2, TPC])
        rs = sb("rs", [P, 2, TPC])
        nb = sb("nb", [P, TPC])
        xn = sb("xn", [P, TPC, P])
        xnT = sb("xnT", [P, CHUNK])
        q_sb = sb("q_sb", [P, CHUNK])
        k_sb = sb("k_sb", [P, CHUNK])
        vo_sb = sb("vo_sb", [P, TPC, P])
        smax = sb("smax", [P, TPC])
        sc = sb("sc", [P, TPC, P // 2])
        prob = sb("prob", [P, TPC, P])
        pT = sb("pT", [P, CHUNK])
        den = sb("den", [P, TPC])
        st2 = sb("st2", [P, TPC, 6])
        tn_sb = sb("tn_sb", [P, TPC, D])
        tnT = sb("tnT", [P, CHUNK])
        best = sb("best", [P, TPC, 8])
        best_i = sb("best_i", [P, TPC, 8], U32)
        dm = sb("dm", [P, NT])
        ex = sb("ex", [P, NT])
        ex1 = sb("ex1", [P, NT])
        oh = sb("oh", [P, 2, NT, E], BF16)
        both = sb("both", [P, NT, E], BF16)
        cnt = sb("cnt", [P, E, NT])
        upto = sb("upto", [P, E, NT])
        tot_i = sb("tot_i", [P, E], I32)
        cnt_i = sb("cnt_i", [P, E], I32)
        ntile = sb("ntile", [P, E])
        prod = sb("prod", [P, E, E])
        first = sb("first", [P, E])
        base = sb("base", [P, E])
        ends = sb("ends", [P, E])
        done = sb("done", [P, TILES, E], BF16)
        exp_f = sb("exp_f", [P, TILES])
        exp_01 = sb("exp_01", [P, TILES], I32)
        place = sb("place", [P, NT, E])
        pp = sb("pp", [P, 2, NT, E])
        slot = sb("slot", [P, 2, NT])
        slot_i = sb("slot_i", [P, GROUPS, NT, 2], I32)
        hi_i = sb("hi_i", [P, NT, 2], I32)
        lo_i = sb("lo_i", [P, NT, 2], I32)
        hi_f = sb("hi_f", [P, NT, 2])
        lo_f = sb("lo_f", [P, NT, 2])
        sel_p = sb("sel_p", [P, 2, 2, P], F16)
        sel_t = sb("sel_t", [P, 2, 2, TILES], F16)
        src_i = sb("src_i", [P, TILES], I32)
        gidx = sb("gidx", [P, 2, HALF], I32)
        xg = sb("xg", [P, RING, D])
        xgT = sb("xgT", [P, 2, P])
        sil = sb("sil", [P, 2, M])
        hid = sb("hid", [P, 2, M])
        hT = sb("hT", [P, 2, M])
        ys = sb("ys", [P, 2, HALF, D])
        cidx = sb("cidx", [P, 2, 2, 2], I32)
        yg = sb("yg", [P, TPC, 2, D])
        o1 = sb("o1", [P, TPC, D])
        o2 = sb("o2", [P, TPC, D])

        bank = [ctx.enter_context(nc.psum_tensor(f"bank{n}", [P, CHUNK], F32)) for n in range(8)]
        XT, XNT, Q, K, VO, S, PT, Y = bank
        OT, TNT = XT, PT
        LG = XNT[:, 0:TPC * E]
        DN = S[:, 0:TPC]

        def by_tile(b):
            return b[:, :].rearrange("p (j n) -> p j n", j=TPC)

        w_in = sem("w_in"); e_in = sem("e_in"); x_in = [sem(f"x_in{n}") for n in range(GROUPS + 2)]
        pool_c = sem("pool_c"); vec = sem("vec")
        wt_ps = sem("wt_ps"); wt_sb = sem("wt_sb"); wvo_ps = sem("wvo_ps"); wvo_sb = sem("wvo_sb")
        xw_ok = sem("xw_ok")
        xt_ps = sem("xt_ps"); x_ok = sem("x_ok"); 
        stats = sem("stats"); xn_ok = sem("xn_ok")
        xnt_ps = sem("xnt_ps"); xnt_ok = sem("xnt_ok")
        qk_ps = sem("qk_ps"); vo_ps = sem("vo_ps"); qk_ok = sem("qk_ok"); vo_ok = sem("vo_ok")
        s_ps = sem("s_ps"); sc_ok = sem("sc_ok"); p_ok = sem("p_ok")
        pt_ps = sem("pt_ps"); pt_ok = sem("pt_ok")
        y_ps = sem("y_ps"); den_ok = sem("den_ok"); t_ok = sem("t_ok");
        tn_ok = sem("tn_ok"); tn_out = sem("tn_out");
        tnt_ps = sem("tnt_ps"); tnt_ok = sem("tnt_ok")
        lg_ps = sem("lg_ps"); lg_ok = sem("lg_ok")
        both_ok = sem("both_ok"); rank_ps = sem("rank_ps"); cnt_ok = sem("cnt_ok"); dm_ok = sem("dm_ok")
        ex_ok = sem("ex_ok"); exp_ok = sem("exp_ok"); src_ok = sem("src_ok")
        sel_ok = sem("sel_ok"); sel_used = sem("sel_used")
        gidx_ok = sem("gidx_ok"); xg_in = [sem(f"xg_in{u}") for u in range(RING)]
        xgt_ps = sem("xgt_ps"); xgt_ok = sem("xgt_ok")
        h_ps = sem("h_ps"); sil_ok = sem("sil_ok"); hid_ok = sem("hid_ok")
        ht_ps = sem("ht_ps"); ht_ok = sem("ht_ok"); ye_ps = sem("ye_ps"); ye_ok = sem("ye_ok")
        y_out = sem("y_out")
        cidx_ok = sem("cidx_ok"); yg_in = [sem(f"yg_in{j}") for j in range(TPC)]
        o_ok = sem("o_ok"); ot_ps = sem("ot_ps"); ot_half = sem("ot_half"); ot_ok = sem("ot_ok"); o_out = sem("o_out")
        NCONST = 14

        block = ctx.enter_context(nc.Block())

        def wait_apart(eng, *waits):
            waits = [(s, v if isinstance(v, int) else eng.to_reg(v)) for s, v in waits]
            eng.wait_ge(pool_c, NCONST)
            for s, v in waits:
                eng.wait_ge(s, v)

        def wait_past(eng, s, v):
            if not (isinstance(v, int) and v <= 0):
                eng.wait_ge(s, v)

        def by_window(a):
            return a.rearrange("c a (s h w k) -> c (a s) w h k", h=WS, w=W // WS, k=WS)

        def conv_steps(eng, g, step, ticks=None):
            def at(i, k):
                return k <= i < NCH + k
            lo = LAG if g > 0 or ticks is not None else LAG + 1
            for i in range(STEPS):
                if i < lo or i >= NCH - 1:
                    step(i, g * NCH + i, [at(i, k) for k in range(LAG + 1)], g > 0 and at(i, 1), g > 0 and at(i, 2))
                elif i == lo:
                    looped(eng, lo, NCH - 1, lambda i: step(i, g * NCH + i, [True] * (LAG + 1), g > 0, g > 0), ticks)

        def looped(eng, lo, hi, body, ticks=None):
            if ticks is None:
                with eng.Fori(lo, hi) as i:
                    body(i)
                return
            ticks.base, ticks.count = ticks.now(), 0
            start = ticks.base
            body(lo)
            per = ticks.count
            with eng.Fori(lo + 1, hi) as i:
                ticks.base, ticks.count = (i - lo) * per + start, 0
                body(i)
                assert ticks.count == per
            ticks.base, ticks.count = start + per * (hi - lo), 0

        @block.sync
        def _(sp):
            x_v = x.rearrange("b c (s h) w -> c b s (h w)", s=SPB)
            x_s = x_sb[:, :, :].rearrange("c (b s) t -> c b s t", s=SPB)
            out_v = out.rearrange("b c (s h) w -> c b s (h w)", s=SPB)
            sp.dma_start(x_s[:, 0, 0, :], x_v[:, 0, 0, :]).then_inc(x_in[0], 16)
            for n, w in enumerate((wq, wk, wo, wv)):
                sp.dma_start(raw[:, n, :], w).then_inc(w_in, 16)
            sp.dma_start(bo_row[:, :], bo.rearrange("(a c) -> a c", a=1)).then_inc(w_in, 16)
            for n, b in enumerate((bq, bk, bv)):
                sp.dma_start(bcols[:, n:n + 1], b.rearrange("(c a) -> c a", a=1)).then_inc(w_in, 16)
            sp.dma_start(x_s[:, 0, 1:SPB, :], x_v[:, 0, 1:SPB, :]).then_inc(x_in[1], 16)
            sp.dma_start(wg_sb[:, :], wg).then_inc(w_in, 16)
            half = B // GROUPS
            sp.dma_start(x_s[:, 1:half, :, :].rearrange("c b s t -> c b (s t)"),
                         x_v[:, 1:half, :, :].rearrange("c b s t -> c b (s t)")).then_inc(x_in[2], 16)
            for g in range(1, GROUPS):
                sp.dma_start(x_s[:, g * half:(g + 1) * half, :, :].rearrange("c b s t -> c b (s t)"),
                             x_v[:, g * half:(g + 1) * half, :, :].rearrange("c b s t -> c b (s t)")
                             ).then_inc(x_in[g + 2], 16)
            sp.dma_start(w01[:, :, 0, :], w0.rearrange("e d m -> d e m")).then_inc(e_in, 16)
            sp.dma_start(w01[:, :, 1, :], w1.rearrange("e d m -> d e m")).then_inc(e_in, 16)
            sp.dma_start(w2_sb[:, :, :, :], w2.rearrange("e (k m) d -> m e k d", k=2)).then_inc(e_in, 16)

            def tn_store(g, n):
                sp.wait_ge(tn_ok, n + 1)
                rows = tn_dram[g].rearrange("(n j p) d -> p n j d", p=P, j=TPC)
                sp.dma_start(rows[:, bass.ds(n - g * NCH, 1), :, :], tn_sb[:, :, :].unsqueeze(1)).then_inc(tn_out, 16)

            def out_store(n):
                wait_apart(sp, (ot_ok, n + 1))
                dst = out.rearrange("b c (s h) w -> c b s (h w)", s=SPB)
                sp.dma_start(dst[:, bass.ds(n // SPB, 1), bass.ds(n % SPB, 1), :],
                             x_sb[:, bass.ds(n, 1), :].unsqueeze(1)).then_inc(o_out, 16)

            def step(g):
                def run(i, n, live, back, turn):
                    if turn:
                        out_store(n - NCH - 2)
                    if live[3]:
                        tn_store(g, n - 3)
                return run

            def y_store(g, r, half):
                n = (g * ROUNDS + r) * 2 + half
                sp.wait_ge(ye_ok, (n + 1) * HALF)
                rows = y_dram[g].rearrange("(r a u p) d -> p r a u d", p=P, a=2, u=HALF)
                sp.dma_start(rows[:, bass.ds(r, 1), half, :, :], ys[:, half:half + 1, :, :]).then_inc(y_out, 16)
                wait_apart(sp, (y_out, (n + 1) * 16))

            def y_round(g):
                def run(r):
                    y_store(g, r, 0)
                    y_store(g, r, 1)
                return run

            for g in range(GROUPS):
                conv_steps(sp, g, step(g))
                looped(sp, 0, ROUNDS, y_round(g))
            looped(sp, (GROUPS - 1) * NCH, GROUPS * NCH, out_store)
            sp.wait_ge(tn_out, GROUPS * NCH * 16)
            sp.wait_ge(y_out, GROUPS * ROUNDS * 32)
            sp.wait_ge(o_out, GROUPS * NCH * 16)

        @block.gpsimd
        def _(pool):
            made = Ticks()

            def make(ins):
                ins.then_inc(pool_c, 1)
                made.up()

            def count(dst, pattern, base_=0, per_partition=0):
                make(pool.iota(dst, pattern, base=base_, channel_multiplier=per_partition,
                               allow_small_or_imprecise_dtypes=True))

            make(pool.memset(ident[:, :], 0.0))
            make(pool.memset(ones_f[:, :], 1.0))
            make(pool.memset(ones_b[:, :], 1.0))
            make(pool.memset(earlier[:, :, :], 1.0))
            make(pool.memset(ones_row[:, :], 1.0))
            make(pool.memset(inside[:, :, :], 1.0))
            make(pool.memset(eps[:, 0, :], LN_C_EPS))
            make(pool.memset(eps[:, 1, :], LN_T_EPS))
            pool.wait_ge(pool_c, made.now())
            make(pool.affine_select(out=ident[:, :], in_=ident[:, :], compare_op=ALU.not_equal, fill=1.0,
                                    base=0, pattern=[[-1, P]], channel_multiplier=1))
            make(pool.affine_select(out=before_b[:, :], in_=ones_b[:, :], compare_op=ALU.is_gt, fill=0.0,
                                    base=0, pattern=[[1, P]], channel_multiplier=-1))
            make(pool.affine_select(out=earlier[:, :, :], in_=earlier[:, :, :], compare_op=ALU.is_gt, fill=0.0,
                                    base=0, pattern=[[1, E], [-1, E]], channel_multiplier=0))
            make(pool.affine_select(out=inside[:, :, :], in_=inside[:, :, :], compare_op=ALU.is_gt, fill=0.0,
                                    base=0, pattern=[[0, E], [1, NT]], channel_multiplier=0))
            count(token_id[:, :], [[P, NT]], base_=-MID, per_partition=1)
            count(iota_e[:, :], [[1, E]])
            assert made.now() == NCONST
            count(iota_p[:, :], [[1, P]])
            count(iota_t[:, :], [[1, TILES]])
            count(iota_te[:, :, :], [[1, TILES], [0, E]])

            def gather_half(g, r, half, opening=False):
                n = g * ROUNDS + r
                us = range(half * HALF, (half + 1) * HALF)
                if not opening:
                    for u in us:
                        pool.wait_ge(xg_in[u], n * 16)
                pool.tensor_copy(gidx[:, half, :], src_i[:, bass.ds(r * RING + half * HALF, HALF)]).then_inc(gidx_ok, 1)
                for u in us:
                    free = [] if opening else [(xgt_ps, (n - 1) * RING + u + 1)]
                    wait_apart(pool, (gidx_ok, n * 2 + half + 1), *free)
                    pool.indirect_dma_start(
                        out=xg[:, u, :], out_offset=None, in_=tn_dram[g],
                        in_offset=bass.IndirectOffsetOnAxis(ap=gidx[:, half, u % HALF:u % HALF + 1], axis=0)
                    ).then_inc(xg_in[u], 16)

            def gather_round(g):
                def run(r, opening=False):
                    gather_half(g, r, 0, opening)
                    gather_half(g, r, 1, opening)
                return run

            def gather_back(g):
                def run(i, opening=False):
                    n = g * NCH + i
                    for half in range(2):
                        js = range(half * 2, half * 2 + 2)
                        if not opening:
                            for j in js:
                                pool.wait_ge(yg_in[j], n * 32)
                        pool.tensor_copy(cidx[:, half, :, :],
                                         slot_i[:, g, bass.ds(i * TPC + half * 2, 2), :]).then_inc(cidx_ok, 1)
                        free = [] if opening else [(o_ok, (n - 1) * 2 + half + 1)]
                        wait_apart(pool, (cidx_ok, n * 2 + half + 1), *free)
                        for j in js:
                            for k in range(2):
                                pool.indirect_dma_start(
                                    out=yg[:, j, k, :], out_offset=None, in_=y_dram[g],
                                    in_offset=bass.IndirectOffsetOnAxis(ap=cidx[:, half, j % 2, k:k + 1], axis=0)
                                ).then_inc(yg_in[j], 16)
                return run

            for g in range(GROUPS):
                pool.wait_ge(src_ok, g + 1)
                pool.wait_ge(tn_out, (g + 1) * NCH * 16)
                gather_round(g)(0, opening=(g == 0))
                looped(pool, 1, ROUNDS, gather_round(g))
                pool.wait_ge(y_out, (g + 1) * ROUNDS * 32)
                gather_back(g)(0, opening=(g == 0))
                looped(pool, 1, NCH, gather_back(g))

        @block.tensor
        def _(pe):
            def transposes(dst, srcs, ready):
                for j, s in enumerate(srcs):
                    mm = pe.transpose(dst[:, j * P:(j + 1) * P], s, ident[:, :])
                mm.then_inc(ready, 1)

            tiles = [slice(j * P, (j + 1) * P) for j in range(TPC)]

            pe.wait_ge(pool_c, NCONST)
            pe.wait_ge(w_in, 9 * 16)
            transposes(Q, [raw[:, n, :] for n in range(3)], wt_ps)
            pe.wait_ge(wt_sb, 2)
            pe.matmul(K[:, 0:P], raw[:, 3, :], woT[:, :], start=True, stop=True)
            pe.matmul(K[:, P:2 * P], bv_b[:, :], woT[:, :], start=True, stop=False)
            pe.matmul(K[:, P:2 * P], ones_row[:, :], bo_row[:, :], start=False, stop=True).then_inc(wvo_ps, 1)
            pe.wait_ge(wvo_sb, 4)

            def step(g):
                def run(i, n, live, back, turn):
                    if live[0]:
                        wait_past(pe, xw_ok, 2 * n + 2)
                        wait_past(pe, x_ok, n)
                        if g > 0:
                            wait_past(pe, ot_ok, (g - 1) * NCH + i - 2)
                        transposes(XT, [xw[:, t] for t in tiles], xt_ps)
                    if live[2]:
                        pe.wait_ge(qk_ok, 2 * (n - 1))
                        wait_past(pe, den_ok, n - 2)
                        for t in tiles:
                            mm = pe.matmul(S[:, t], q_sb[:, t], k_sb[:, t], start=True, stop=True)
                        mm.then_inc(s_ps, 1)
                    if live[1]:
                        pe.wait_ge(xn_ok, n)
                        wait_past(pe, lg_ok, n - 3)
                        transposes(XNT, [xn[:, j, :] for j in range(TPC)], xnt_ps)
                    if live[1]:
                        pe.wait_ge(xnt_ok, n)
                        wait_past(pe, qk_ok, 2 * (n - 1))
                        pe.matmul(Q[:, :], wqT[:, :], xnT[:, :], start=True, stop=True)
                        pe.matmul(K[:, :], wkT[:, :], xnT[:, :], start=True, stop=True).then_inc(qk_ps, 1)
                        wait_past(pe, vo_ok, n - 1)
                        for t in tiles:
                            mm = pe.matmul(VO[:, t], xnT[:, t], wvo[:, :], start=True, stop=True)
                        mm.then_inc(vo_ps, 1)
                    if live[3]:
                        pe.wait_ge(tn_ok, n - 2)
                        transposes(TNT, [tn_sb[:, j, :] for j in range(TPC)], tnt_ps)
                    if turn:
                        pe.wait_ge(x_ok, n + 1 if live[0] else (g + 1) * NCH)
                        turn_back(n - NCH - 2)
                    if live[2]:
                        pe.wait_ge(p_ok, n - 1)
                        if live[3]:
                            pe.wait_ge(tnt_ok, n - 2)
                        transposes(PT, [prob[:, j, :] for j in range(TPC)], pt_ps)
                    if live[3]:
                        pe.wait_ge(tnt_ok, n - 2)
                        if not live[1]:
                            wait_past(pe, lg_ok, n - 3)
                        for j, t in enumerate(tiles):
                            mm = pe.matmul(LG[:, j * E:(j + 1) * E], tnT[:, t], wg_sb[:, :], start=True, stop=True)
                        mm.then_inc(lg_ps, 1)
                    if live[2]:
                        pe.wait_ge(pt_ok, n - 1)
                        pe.wait_ge(vo_ok, n - 1)
                        wait_past(pe, t_ok, n - 2)
                        for j, t in enumerate(tiles):
                            pe.matmul(DN[:, j:j + 1], pT[:, t], ones_f[:, 0:1], start=True, stop=True)
                            mm = pe.matmul(Y[:, t], pT[:, t], vo_sb[:, j, :], start=True, stop=True)
                        mm.then_inc(y_ps, 1)
                return run

            def turn_back(n):
                pe.wait_ge(o_ok, 2 * (n + 1))
                transposes(OT, [o2[:, j, :] for j in range(TPC)], ot_ps)

            w01_v = w01[:, :, :, :].rearrange("p e a m -> p (e a m)")
            w2_v = w2_sb[:, :, :, :].rearrange("p e k d -> p (e k d)")

            expert_of = [pe.alloc_register(f"expert_of_tile{u}") for u in range(RING)]

            def load_experts(r, half):
                pe.load(expert_of[half * HALF:(half + 1) * HALF],
                        exp_01[0:1, bass.ds(r * RING + half * HALF, HALF)])

            def expert(u):
                return pe.snap(expert_of[u % RING], min_val=0, max_val=(E - 1) * 2 * M)

            def expert_round(g, r, start=False, end=False):
                n0 = (g * ROUNDS + r) * RING

                def turn_x(u):
                    n = n0 + u
                    pe.wait_ge(xg_in[u % RING], (g * ROUNDS + r + u // RING + 1) * 16)
                    wait_past(pe, xgt_ok, n - 1)
                    pe.transpose(bank[u % 2][:, 0:P], xg[:, u % RING, :], ident[:, :]).then_inc(xgt_ps, 1)

                def hidden(u, at):
                    n = n0 + u
                    pe.wait_ge(xgt_ok, n + 1)
                    wait_past(pe, hid_ok, n - 1)
                    pe.matmul(bank[2 + u % 2][:, :], xgT[:, u % 2, :], w01_v[:, bass.ds(at, 2 * M)],
                              start=True, stop=True).then_inc(h_ps, 1)

                def turn_h(u):
                    n = n0 + u
                    pe.wait_ge(hid_ok, n + 1)
                    wait_past(pe, ht_ok, n - 1)
                    pe.transpose(bank[4 + u % 2][:, 0:P], hid[:, u % 2, 0:P], ident[:, :])
                    pe.transpose(bank[4 + u % 2][:, P:M], hid[:, u % 2, P:M], ident[:, :]).then_inc(ht_ps, 1)

                def down(u, at):
                    n = n0 + u
                    pe.wait_ge(ht_ok, n + 1)
                    wait_past(pe, ye_ok, n - 1)
                    at = at // 2
                    pe.matmul(bank[6 + u % 2][:, 0:D], hT[:, u % 2, 0:P], w2_v[:, bass.ds(at, D)],
                              start=True, stop=False)
                    pe.matmul(bank[6 + u % 2][:, 0:D], hT[:, u % 2, P:M], w2_v[:, bass.ds(at + D, D)],
                              start=False, stop=True).then_inc(ye_ps, 1)

                if start:
                    load_experts(r, 0)
                    turn_x(0)
                for u in range(RING):
                    if not (end and u == RING - 1):
                        turn_x(u + 1)
                    hidden(u, expert(u))
                    if u == 2:
                        load_experts(r, 1)
                    if u == HALF + 2 and not end:
                        load_experts(r + 1, 0)
                    if not (start and u < 2):
                        down(u - 2, expert(u - 2))
                    if not (start and u < 1):
                        turn_h(u - 1)
                if end:
                    down(RING - 2, expert(RING - 2))
                    turn_h(RING - 1)
                    down(RING - 1, expert(RING - 1))

            for g in range(GROUPS):
                conv_steps(pe, g, step(g))
                pe.wait_ge(qk_ok, 2 * (g + 1) * NCH)
                pe.wait_ge(both_ok, g + 1)
                both_v = both[:, :, :].rearrange("p j e -> p (j e)")
                pe.matmul(K[:, :], ones_b[:, :], both_v, start=True, stop=True)
                pe.matmul(Q[:, :], before_b[:, :], both_v, start=True, stop=True).then_inc(rank_ps, 1)
                pe.wait_ge(cnt_ok, g + 1)

                def pick(i, b, first_=False, last=False):
                    pe.wait_ge(sel_ok, g * NT + i + 1)
                    for k in range(2):
                        mm = pe.matmul(K[:, 0:TILES], sel_p[:, b, k, :], sel_t[:, b, k, :],
                                       start=(first_ and k == 0), stop=(last and k == 1))
                    mm.then_inc(sel_used, 1)

                def picks(i2):
                    pick(i2 * 2, 0)
                    pick(i2 * 2 + 1, 1)
                pick(0, 0, first_=True)
                pick(1, 1)
                looped(pe, 1, NT // 2 - 1, picks)
                pick(NT - 2, 0)
                pick(NT - 1, 1, last=True)
                pe.wait_ge(src_ok, g + 1)
                if g == 0:
                    pe.wait_ge(e_in, 3 * 16)
                pe.wait_ge(exp_ok, g + 1)
                pe.wait_ge(ot_ok, g * NCH) if g > 0 else None
                expert_round(g, 0, start=True)
                looped(pe, 1, ROUNDS - 1, lambda r: expert_round(g, r))
                expert_round(g, ROUNDS - 1, end=True)
                pe.wait_ge(ye_ok, (g + 1) * TILES)

            def last_turn(n):
                pe.wait_ge(ot_ok, n)
                turn_back(n)
            looped(pe, (GROUPS - 1) * NCH, GROUPS * NCH, last_turn)

        @block.scalar
        def _(act):
            def out_copy(n):
                act.wait_ge(ot_ps, n + 1)
                dst = by_window(x_sb[:, bass.ds(n, 1), :])
                src = OT[:, :].rearrange("c (s w h k) -> c s w h k", s=CHUNK // W // WS, h=WS, k=WS)
                act.copy(dst[:, 0, :, :, :], src[:, 0, :, :, :]).then_inc(ot_half, 1)
                act.copy(dst[:, 1, :, :, :], src[:, 1, :, :, :]).then_inc(ot_ok, 1)

            def window_order(n):
                src = by_window(x_sb[:, bass.ds(n, 1), :])
                dst = xw[:, :].rearrange("c (s w h k) -> c s w h k", w=W // WS, h=WS, k=WS)
                for s in range(2):
                    act.copy(dst[:, s, :, :, :], src[:, s, :, :, :]).then_inc(xw_ok, 1)

            def step(g):
                def run(i, n, live, back, turn):
                    if live[0]:
                        act.wait_ge(xt_ps, n + 1)
                        act.copy(t_sb[:, bass.ds(n * TPC, TPC), :], by_tile(XT)).then_inc(x_ok, 1)
                        if not (isinstance(i, int) and i == NCH - 1 and g == GROUPS - 1):
                            window_order(n + 1)
                    if live[2]:
                        act.wait_ge(sc_ok, n - 1)
                        wait_past(act, pt_ps, n - 2)
                        h = P // 2
                        act.activation(prob[0:h, :, 0:h], sc[0:h, :, :], ACT.Exp, scale=SCALE)
                        act.activation(prob[h:P, :, h:P], sc[h:P, :, :], ACT.Exp, scale=SCALE).then_inc(p_ok, 1)
                    if live[1]:
                        act.wait_ge(xnt_ps, n)
                        wait_past(act, vo_ps, n - 1)
                        act.copy(xnT[:, :], XNT[:, :]).then_inc(xnt_ok, 1)
                    if live[1]:
                        act.wait_ge(qk_ps, n)
                        wait_past(act, s_ps, n - 1)
                        act.activation(q_sb[:, :], Q[:, :], ACT.Identity, bias=bcols[:, 0:1]).then_inc(qk_ok, 1)
                        act.activation(k_sb[:, :], K[:, :], ACT.Identity, bias=bcols[:, 1:2]).then_inc(qk_ok, 1)
                    if live[0]:
                        used = [] if isinstance(n, int) and n == 0 else [(xnt_ps, n)]
                        wait_apart(act, (stats, n + 1), *used)
                        for j in range(TPC):
                            rows = t_sb[:, bass.ds(n * TPC + j, 1), :].rearrange("p a d -> p (a d)")
                            ins = act.activation(xn[:, j, :], rows, ACT.Identity, bias=nb[:, j:j + 1],
                                                 scale=rs[:, 0, j:j + 1])
                        ins.then_inc(xn_ok, 1)
                    if live[3]:
                        act.wait_ge(tnt_ps, n - 2)
                        wait_past(act, lg_ps, n - 3)
                        act.copy(tnT[:, :], TNT[:, :]).then_inc(tnt_ok, 1)
                    if turn:
                        out_copy(n - NCH - 2)
                    if live[2]:
                        act.wait_ge(pt_ps, n - 1)
                        wait_past(act, y_ps, n - 2)
                        act.copy(pT[:, :], PT[:, :]).then_inc(pt_ok, 1)
                return run

            def x_copy(n0, u):
                n = n0 + u
                act.wait_ge(xgt_ps, n + 1)
                wait_past(act, h_ps, n - 1)
                act.copy(xgT[:, u % 2, :], bank[u % 2][:, 0:P]).then_inc(xgt_ok, 1)

            def silu(n0, u):
                n = n0 + u
                act.wait_ge(h_ps, n + 1)
                wait_past(act, hid_ok, n - 1)
                act.activation(sil[:, u % 2, :], bank[2 + u % 2][:, 0:M], ACT.Silu).then_inc(sil_ok, 1)

            def expert_round(g, r, start=False, end=False):
                n0 = (g * ROUNDS + r) * RING
                if start:
                    x_copy(n0, 0)
                for u in range(RING):
                    if not (end and u == RING - 1):
                        x_copy(n0, u + 1)
                    silu(n0, u)

            act.wait_ge(x_in[0], 16)
            window_order(0)
            for q in x_in[1:3]:
                act.wait_ge(q, 16)
            for g in range(GROUPS):
                if g + 1 < GROUPS:
                    act.wait_ge(x_in[g + 3], 16)
                conv_steps(act, g, step(g))
                act.wait_ge(dm_ok, g + 1)
                act.activation(ex[:, :], dm[:, :], ACT.Exp).then_inc(ex_ok, 1)
                act.wait_ge(rank_ps, g + 1)
                act.copy(cnt[:, :, :].rearrange("p e j -> p j e"),
                         K[:, :].rearrange("p (j e) -> p j e", e=E)).then_inc(cnt_ok, 1)
                expert_round(g, 0, start=True)
                looped(act, 1, ROUNDS - 1, lambda r: expert_round(g, r))
                expert_round(g, ROUNDS - 1, end=True)
            looped(act, (GROUPS - 1) * NCH, GROUPS * NCH, out_copy)

        @block.vector
        def _(dve):
            tick = Ticks()

            def then(ins):
                ins.then_inc(vec, 1)
                tick.up()

            def settled():
                dve.wait_ge(vec, tick.now())

            def chain(ins):
                then(ins)
                settled()

            dve.wait_ge(pool_c, NCONST)
            then(dve.memset(prob[:, :, :], 0.0))
            dve.wait_ge(w_in, 9 * 16)
            dve.tensor_copy(bv_b[:, :], bcols[:, 2:3].to_broadcast([P, P])).then_inc(wt_sb, 1)
            dve.wait_ge(wt_ps, 1)
            dve.tensor_copy(woT[:, :], Q[:, 2 * P:3 * P]).then_inc(wt_sb, 1)
            dve.tensor_copy(wqT[:, :], Q[:, 0:P]).then_inc(wvo_sb, 1)
            dve.tensor_copy(wkT[:, :], Q[:, P:2 * P]).then_inc(wvo_sb, 1)
            dve.wait_ge(wvo_ps, 1)
            dve.tensor_copy(wvo[:, :], K[:, 0:P]).then_inc(wvo_sb, 1)
            dve.tensor_copy(bvo[:, :], K[:, P:2 * P]).then_inc(wvo_sb, 1)
            dve.wait_ge(wvo_sb, 4)
            settled()

            def moments(rows, st_, k):
                for j in range(TPC):
                    then(dve.bn_stats(st_[:, j, :], rows[j]))
                wait_apart(dve, (vec, tick.now()))
                for j in range(TPC):
                    then(dve.bn_aggr(mv[:, k, j, :], st_[:, j, :]))

            def roots(k):
                settled()
                chain(dve.tensor_tensor(var[:, k, :], mv[:, k, :, 1], eps[:, k, :], ALU.add))
                chain(dve.tensor_scalar(bits[:, k, :], var[:, k, :].bitcast(I32), 1, None, ALU.logical_shift_right))
                chain(dve.tensor_scalar(rs[:, k, :].bitcast(I32), bits[:, k, :], -1.0, float(0x5f3759df),
                                        ALU.mult, ALU.add))
                for _ in range(3):
                    chain(dve.tensor_tensor(sq[:, k, :], rs[:, k, :], rs[:, k, :], ALU.mult))
                    chain(dve.scalar_tensor_tensor(out=sq[:, k, :], in0=sq[:, k, :], scalar=-0.5, in1=var[:, k, :],
                                                   op0=ALU.mult, op1=ALU.mult))
                    chain(dve.scalar_tensor_tensor(out=rs[:, k, :], in0=sq[:, k, :], scalar=1.5, in1=rs[:, k, :],
                                                   op0=ALU.add, op1=ALU.mult))

            def token_rows(n, j):
                return t_sb[:, bass.ds(n * TPC + j, 1), :].rearrange("p a d -> p (a d)")

            def combine(n, half):
                js = (half * 2, half * 2 + 1)
                for j in js:
                    dve.wait_ge(yg_in[j], (n + 1) * 32)
                for j in js:
                    then(dve.scalar_tensor_tensor(out=o1[:, j, :], in0=yg[:, j, 0, :],
                                                  scalar=gate[:, 0, bass.ds(n * TPC + j, 1)],
                                                  in1=token_rows(n, j), op0=ALU.mult, op1=ALU.add))
                settled()
                wait_past(dve, ot_ps, n)
                for j in js:
                    ins = dve.scalar_tensor_tensor(out=o2[:, j, :], in0=yg[:, j, 1, :],
                                                   scalar=gate[:, 1, bass.ds(n * TPC + j, 1)],
                                                   in1=o1[:, j, :], op0=ALU.mult, op1=ALU.add)
                    if j == js[0]:
                        then(ins)
                ins.then_inc(o_ok, 1)

            def step(g):
                def run(i, n, live, back, turn):
                    if live[2]:
                        dve.wait_ge(s_ps, n - 1)
                        h = P // 2
                        sv = by_tile(S)
                        then(dve.tensor_reduce(smax[0:h, :], sv[0:h, :, 0:h], AX.X, ALU.max))
                        then(dve.tensor_reduce(smax[h:P, :], sv[h:P, :, h:P], AX.X, ALU.max))
                        settled()
                        wait_past(dve, p_ok, n - 2)
                        then(dve.tensor_tensor(sc[0:h, :, :], sv[0:h, :, 0:h],
                                               smax[0:h, :].unsqueeze(2).to_broadcast([h, TPC, h]), ALU.subtract))
                        dve.tensor_tensor(sc[h:P, :, :], sv[h:P, :, h:P],
                                          smax[h:P, :].unsqueeze(2).to_broadcast([h, TPC, h]),
                                          ALU.subtract).then_inc(sc_ok, 1)
                    if live[0]:
                        wait_apart(dve, (x_ok, n + 1))
                        moments([token_rows(n, j) for j in range(TPC)], st, 0)
                        wait_past(dve, xn_ok, n)
                    if live[0] or live[3]:
                        roots(slice(0 if live[0] else 1, 2 if live[3] else 1))
                    if live[0]:
                        dve.scalar_tensor_tensor(out=nb[:, :], in0=mv[:, 0, :, 0], scalar=-1.0, in1=rs[:, 0, :],
                                                 op0=ALU.mult, op1=ALU.mult).then_inc(stats, 1)
                    if live[3]:
                        m = n - 3
                        wait_past(dve, tnt_ps, m)
                        wait_past(dve, tn_out, m * 16)
                        for j in range(TPC):
                            ins = dve.tensor_scalar(tn_sb[:, j, :], token_rows(m, j), mv[:, 1, j, 0:1],
                                                    rs[:, 1, j:j + 1], ALU.subtract, ALU.mult)
                            if j < TPC - 1:
                                then(ins)
                        ins.then_inc(tn_ok, 1)
                    if live[3]:
                        m = n - 3
                        wait_apart(dve, (lg_ps, m + 1))
                        for j in range(TPC):
                            then(dve.max(best[:, j, :], LG[:, j * E:(j + 1) * E]))
                        wait_apart(dve, (vec, tick.now()))
                        for j in range(TPC):
                            ins = dve.max_index(best_i[:, j, :], best[:, j, :], LG[:, j * E:(j + 1) * E])
                            if j < TPC - 1:
                                then(ins)
                        ins.then_inc(lg_ok, 1)
                        own = bass.ds((m - g * NCH) * TPC, TPC)
                        then(dve.tensor_copy(top_v[:, own, :], best[:, :, 0:2]))
                        dve.wait_ge(lg_ok, m + 1)
                        settled()
                        then(dve.tensor_copy(top_e[:, own, :], best_i[:, :, 0:2]))
                    if back:
                        combine(n - NCH - 1, 0)
                    if live[2]:
                        m = n - 2
                        dve.wait_ge(y_ps, m + 1)
                        dve.reciprocal(den[:, :], DN).then_inc(den_ok, 1)
                        dve.wait_ge(den_ok, m + 1)
                        rows = [token_rows(m, j) for j in range(TPC)]
                        for j in range(TPC):
                            ins = dve.scalar_tensor_tensor(out=rows[j], in0=Y[:, tile_cols(j)],
                                                           scalar=den[:, j:j + 1], in1=rows[j],
                                                           op0=ALU.mult, op1=ALU.add)
                            if j < TPC - 1:
                                then(ins)
                        ins.then_inc(t_ok, 1)
                        wait_apart(dve, (t_ok, m + 1), (vec, tick.now()))
                        moments(rows, st2, 1)
                    if live[1]:
                        dve.wait_ge(vo_ps, n)
                        wait_past(dve, y_ps, n - 1)
                        dve.tensor_tensor(vo_sb[:, :, :], by_tile(VO), bvo[:, :].unsqueeze(1).to_broadcast([P, TPC, P]),
                                          ALU.add).then_inc(vo_ok, 1)
                    if back:
                        combine(n - NCH - 1, 1)
                return run

            def tile_cols(j):
                return slice(j * P, (j + 1) * P)

            def route(g):
                settled()
                for k in range(2):
                    then(dve.tensor_tensor(oh[:, k, :, :], iota_e[:, :].unsqueeze(1).to_broadcast([P, NT, E]),
                                           top_e[:, :, k].unsqueeze(2).to_broadcast([P, NT, E]), ALU.is_equal))
                settled()
                dve.tensor_tensor(both[:, :, :], oh[:, 0, :, :], oh[:, 1, :, :], ALU.add).then_inc(both_ok, 1)
                dve.tensor_tensor(dm[:, :], top_v[:, :, 1], top_v[:, :, 0], ALU.subtract).then_inc(dm_ok, 1)
                dve.wait_ge(ex_ok, g + 1)
                own = slice(g * NT, (g + 1) * NT)
                chain(dve.tensor_scalar(ex1[:, :], ex[:, :], 1.0, None, ALU.add))
                chain(dve.reciprocal(gate[:, 0, own], ex1[:, :]))
                then(dve.tensor_tensor(gate[:, 1, own], gate[:, 0, own], ex[:, :], ALU.mult))
                dve.wait_ge(cnt_ok, g + 1)
                flat = "p e j -> p (e j)"
                chain(dve.tensor_tensor_scan(upto[:, :, :].rearrange(flat), inside[:, :, :].rearrange(flat),
                                             cnt[:, :, :].rearrange(flat), 0.0, ALU.mult, ALU.add))
                chain(dve.tensor_scalar(tot_i[:, :], upto[:, :, NT - 1], float(P - 1), None, ALU.add))
                chain(dve.tensor_scalar(cnt_i[:, :], tot_i[:, :], 7, None, ALU.logical_shift_right))
                chain(dve.tensor_copy(ntile[:, :], cnt_i[:, :]))
                chain(dve.tensor_tensor(prod[:, :, :], earlier[:, :, :],
                                        ntile[:, :].unsqueeze(1).to_broadcast([P, E, E]), ALU.mult))
                chain(dve.tensor_reduce(first[:, :], prod[:, :, :], AX.X, ALU.add))
                then(dve.tensor_tensor(ends[:, :], first[:, :], ntile[:, :], ALU.add))
                then(dve.tensor_scalar(base[:, :], first[:, :], float(P), None, ALU.mult))
                chain(dve.tensor_tensor(upto[:, :, :], upto[:, :, :], cnt[:, :, :], ALU.subtract))
                chain(dve.tensor_tensor(upto[:, :, :], upto[:, :, :],
                                        base[:, :].unsqueeze(2).to_broadcast([P, E, NT]), ALU.add))
                chain(dve.tensor_tensor(place[:, :, :], Q[:, :].rearrange("p (j e) -> p j e", e=E),
                                        upto[:, :, :].rearrange("p e j -> p j e"), ALU.add))
                for k in range(2):
                    then(dve.tensor_tensor(pp[:, k, :, :], place[:, :, :], oh[:, k, :, :], ALU.mult))
                settled()
                chain(dve.tensor_reduce(slot[:, :, :], pp[:, :, :, :], AX.X, ALU.add))
                chain(dve.tensor_copy(slot_i[:, g, :, :].rearrange("p j k -> p k j"), slot[:, :, :]))
                then(dve.tensor_scalar(hi_i[:, :, :], slot_i[:, g, :, :], 7, None, ALU.logical_shift_right))
                chain(dve.tensor_scalar(lo_i[:, :, :], slot_i[:, g, :, :], P - 1, None, ALU.bitwise_and))
                then(dve.tensor_copy(hi_f[:, :, :], hi_i[:, :, :]))
                chain(dve.tensor_copy(lo_f[:, :, :], lo_i[:, :, :]))

                def pick_rows(i, b):
                    n = g * NT + i
                    wait_past(dve, sel_used, n - 1)
                    col = bass.ds(i, 1)
                    for k in range(2):
                        lo, hi = (v[:, col, k:k + 1].rearrange("p a b -> p (a b)") for v in (lo_f, hi_f))
                        then(dve.tensor_scalar(sel_p[:, b, k, :], iota_p[:, :], lo, None, ALU.is_equal))
                        ins = dve.tensor_scalar(sel_t[:, b, k, :], iota_t[:, :], hi, token_id[:, col],
                                                ALU.is_equal, ALU.mult)
                        if k == 0:
                            then(ins)
                    ins.then_inc(sel_ok, 1)

                def pick_two(i2):
                    pick_rows(i2 * 2, 0)
                    pick_rows(i2 * 2 + 1, 1)
                looped(dve, 0, NT // 2, pick_two, tick)
                dve.wait_ge(sel_used, (g + 1) * NT)
                dve.tensor_scalar(src_i[:, :], K[:, 0:TILES], float(MID), None, ALU.add).then_inc(src_ok, 1)
                chain(dve.tensor_tensor(done[:, :, :], iota_te[:, :, :],
                                        ends[:, :].unsqueeze(1).to_broadcast([P, TILES, E]), ALU.is_ge))
                chain(dve.tensor_reduce(exp_f[:, :], done[:, :, :], AX.X, ALU.add))
                chain(dve.tensor_scalar(exp_f[:, :], exp_f[:, :], float(E - 1), None, ALU.min))
                dve.tensor_scalar(exp_01[:, :], exp_f[:, :], float(2 * M), None, ALU.mult).then_inc(exp_ok, 1)

            def experts(g):
                def product(n0, u):
                    n = n0 + u
                    dve.wait_ge(sil_ok, n + 1)
                    wait_past(dve, ht_ps, n - 1)
                    dve.tensor_tensor(hid[:, u % 2, :], sil[:, u % 2, :], bank[2 + u % 2][:, M:2 * M],
                                      ALU.mult).then_inc(hid_ok, 1)

                def y_copy(n0, round_, u):
                    n = n0 + u
                    dve.wait_ge(ye_ps, n + 1)
                    half = (u // HALF) % 2
                    if u % HALF == 0:
                        wait_past(dve, y_out, ((round_ - 1) * 2 + half + 1) * 16)
                    dve.tensor_copy(ys[:, half, u % HALF, :], bank[6 + u % 2][:, 0:D]).then_inc(ye_ok, 1)

                def ht_copy(n0, u):
                    n = n0 + u
                    dve.wait_ge(ht_ps, n + 1)
                    wait_past(dve, ye_ps, n - 1)
                    dve.tensor_copy(hT[:, u % 2, :], bank[4 + u % 2][:, 0:M]).then_inc(ht_ok, 1)

                def one_round(r, start=False):
                    n0 = (g * ROUNDS + r) * RING
                    for u in range(RING):
                        product(n0, u)
                        if not (start and u < 2):
                            y_copy(n0, g * ROUNDS + r, u - 2)
                        if not (start and u < 1):
                            ht_copy(n0, u - 1)
                one_round(0, start=True)
                looped(dve, 1, ROUNDS, one_round)
                n0 = (g + 1) * TILES
                y_copy(n0, None, -2)
                ht_copy(n0, -1)
                y_copy(n0, None, -1)

            for g in range(GROUPS):
                conv_steps(dve, g, step(g), tick)
                if g == 0:
                    dve.wait_ge(pool_c, NCONST + 3)
                route(g)
                experts(g)

            def last_rows(n):
                combine(n, 0)
                combine(n, 1)
            looped(dve, (GROUPS - 1) * NCH, GROUPS * NCH, last_rows, tick)


_INS = ["x", "L0_conv_wq", "L0_conv_bq", "L0_conv_wk", "L0_conv_bk", "L0_conv_wv", "L0_conv_bv",
        "L0_conv_wo", "L0_conv_bo", "L0_ffn_wg", "L0_ffn_w0", "L0_ffn_w1", "L0_ffn_wo"]


def kernel(**inputs):
    import numpy as _np
    import concourse.bacc as _bacc
    from concourse import mybir as _mybir
    from concourse.bass_utils import run_bass_kernel_spmd as _run

    nc = _bacc.Bacc("TRN2", target_bir_lowering=False, num_devices=1)
    arrays, args = {}, []
    for name in _INS:
        a = _np.ascontiguousarray(inputs[name])
        arrays[f"in_{name}"] = a
        args.append(nc.dram_tensor(f"in_{name}", a.shape, _mybir.dt.from_np(a.dtype), kind="ExternalInput").ap())
    shape = inputs["x"].shape
    out = nc.dram_tensor("out_0", shape, _mybir.dt.from_np(_np.dtype("float32")), kind="ExternalOutput").ap()
    emit(nc, *args, out)
    r = _run(nc, [arrays], core_ids=[0])
    return r.results[0]["out_0"]
```

```python
from contextlib import ExitStack

import concourse.bass as bass
from concourse import mybir

F32 = mybir.dt.float32
F32R = mybir.dt.float32r
BF16 = mybir.dt.bfloat16
F16 = mybir.dt.float16
I32 = mybir.dt.int32
U32 = mybir.dt.uint32
ALU = mybir.AluOpType
ACT = mybir.ActivationFunctionType
AX = mybir.AxisListType

P = 128
WS = 8
TPC = 4
CHUNK = TPC * P
RING = 8
HALF = RING // 2
TN_ACT = (2, 3)
LAG = 4


class Ticks:

    def __init__(self):
        self.base, self.count = 0, 0

    def up(self, n=1):
        self.count += n
        return self.base + self.count

    def now(self):
        return self.base + self.count


def emit(nc, x, wq, bq, wk, bk, wv, bv, wo, bo, wg, w0, w1, w2, out):
    B, C, H, W = x.shape
    E, D, M = w0.shape
    assert C == P and D == P and M == 2 * P and H * W % CHUNK == 0
    GROUPS = 2
    NCH = B * H * W // CHUNK // GROUPS
    NT = NCH * TPC
    PAIRS = 2 * NT * P
    TILES = -(-(PAIRS // P + E - 1) // RING) * RING
    ROUNDS = TILES // RING
    MID = NT * P // 2
    assert MID <= 2048
    STEPS = NCH + LAG
    SPB = H * W // CHUNK
    SCALE = float(C) ** -0.5
    LN_C_EPS, LN_T_EPS = 1e-6, 1e-5

    tn_dram = [nc.dram_tensor(f"normed_{g}", (NT * P, D), F32, kind="Internal").ap() for g in range(GROUPS)]
    y_dram = [nc.dram_tensor(f"expert_rows_{g}", (TILES * P, D), F32, kind="Internal").ap() for g in range(GROUPS)]

    with ExitStack() as ctx:
        def sb(name, shape, dt=F32):
            return ctx.enter_context(nc.sbuf_tensor(name, shape, dt))

        def sem(name):
            return ctx.enter_context(nc.semaphore(name))

        ident = sb("ident", [P, P])
        ones_row = sb("ones_row", [1, P])
        ones_f = sb("ones_f", [P, P])
        ones_b = sb("ones_b", [P, P], BF16)
        before_b = sb("before_b", [P, P], BF16)
        earlier = sb("earlier", [P, E, E])
        inside = sb("inside", [P, E, NT], BF16)
        iota_e = sb("iota_e", [P, E])
        token_id = sb("token_id", [P, NT])
        iota_p = sb("iota_p", [P, P], F16)
        iota_t = sb("iota_t", [P, TILES], F16)
        iota_te = sb("iota_te", [P, TILES, E], BF16)
        eps = sb("eps", [P, 2, TPC])
        raw = sb("raw", [P, 4, P])
        wqT = sb("wqT", [P, P])
        wkT = sb("wkT", [P, P])
        wvo = sb("wvo", [P, P])
        bcols = sb("bcols", [P, 3])
        bo_row = sb("bo_row", [1, P])
        bvo_hi = sb("bvo_hi", [1, CHUNK], F32R)
        bvo_lo = sb("bvo_lo", [1, CHUNK], F32R)
        ones_r = sb("ones_r", [1, P], F32R)
        wg_sb = sb("wg_sb", [P, E])
        w01 = sb("w01", [P, E, 2 * M])
        w_hi = sb("w_hi", [P, E, 2 * M], F32R)
        w_lo = w01[:, :, :].bitcast(F32R)
        w2_sb = sb("w2_sb", [P, E, 2 * D])

        x_sb = sb("x_sb", [P, GROUPS * NCH, CHUNK])
        t_sb = sb("t_sb", [P, GROUPS * NT, D])
        top_v = sb("top_v", [P, NT, 2])
        top_e = sb("top_e", [P, NT, 2])
        gate = sb("gate", [P, 2, GROUPS * NT])

        xw = sb("xw", [P, CHUNK])
        st = sb("st", [P, 2, TPC, 6])
        mv = sb("mv", [P, 2, TPC, 2])
        var = sb("var", [P, 2, TPC])
        bits = sb("bits", [P, 2, TPC], I32)
        sq = sb("sq", [P, 2, TPC])
        rs = sb("rs", [P, 2, TPC])
        nb = sb("nb", [P, 2, TPC])
        xn = sb("xn", [P, TPC, P])
        xnT = sb("xnT", [P, CHUNK])
        q_sb = sb("q_sb", [P, CHUNK])
        k_sb = sb("k_sb", [P, CHUNK])
        bv_b, woT = k_sb[:, 0:P], k_sb[:, P:2 * P]
        vo_sb = sb("vo_sb", [P, TPC, P])
        smax = sb("smax", [P, TPC])
        sc = sb("sc", [P, TPC, P // 2])
        prob = sb("prob", [P, TPC, P])
        pT = sb("pT", [P, CHUNK])
        den = sb("den", [P, TPC])
        tn_sb = sb("tn_sb", [P, TPC, D])
        tnT = sb("tnT", [P, CHUNK])
        best = sb("best", [P, TPC, 8])
        best_i = sb("best_i", [P, TPC, 8], U32)

        silu_try = sb("silu_try", [P, 1])
        dm = sb("dm", [P, NT])
        ex = sb("ex", [P, NT])
        ex1 = sb("ex1", [P, NT])
        oh = sb("oh", [P, 2, NT, E], BF16)
        both = sb("both", [P, NT, E], BF16)
        cnt = q_sb[:, :].rearrange("p (e j) -> p e j", e=E)
        upto = k_sb[:, :].rearrange("p (e j) -> p e j", e=E)
        tot_i = sb("tot_i", [P, E], I32)
        cnt_i = sb("cnt_i", [P, E], I32)
        ntile = sb("ntile", [P, E])
        prod = sc[:, :, :].rearrange("p j k -> p (j k)").rearrange("p (e f) -> p e f", e=E)
        first = sb("first", [P, E])
        base = sb("base", [P, E])
        ends = sb("ends", [P, E])
        done = sb("done", [P, TILES, E], BF16)
        exp_f = sb("exp_f", [P, TILES])
        exp_at = sb("exp_at", [P, TILES, 2], I32)
        place = xnT[:, :].rearrange("p (j e) -> p j e", e=E)
        ys = sb("ys", [P, 2, HALF, D])
        pp = ys[:, :, :, :].rearrange("p k u d -> p k (u d)").rearrange("p k (j e) -> p k j e", e=E)
        slot = sb("slot", [P, 2, NT])
        slot_i = sb("slot_i", [P, GROUPS, NT, 2], I32)
        hi_i = sb("hi_i", [P, NT, 2], I32)
        lo_i = sb("lo_i", [P, NT, 2], I32)
        hi_f = sb("hi_f", [P, NT, 2], F16)
        lo_f = sb("lo_f", [P, NT, 2])
        sel_p = sb("sel_p", [P, 2, 2, 2, P], F16)
        sel_t = sb("sel_t", [P, 2, 2, 2, TILES], F16)
        src_i = sb("src_i", [P, TILES], I32)
        gidx = sb("gidx", [P, 2, HALF], I32)
        xg = sb("xg", [P, RING, D])
        x_hi = sb("x_hi", [P, 2, P], F32R)
        x_lo = sb("x_lo", [P, 2, P], F32R)
        sil = xn[:, :, :].rearrange("p (a k) d -> p a (k d)", a=2)
        hid = vo_sb[:, :, :].rearrange("p (a k) d -> p a (k d)", a=2)
        hT = pT[:, :].rearrange("p (a m) -> p a m", a=2)
        cidx = sb("cidx", [P, 2, TPC, 2], I32)
        yg = xg[:, :, :].rearrange("p (j k) d -> p j k d", k=2)
        o1 = raw[:, :, :]
        o2 = sb("o2", [P, TPC, D])

        bank = [ctx.enter_context(nc.psum_tensor(f"bank{n}", [P, CHUNK], F32)) for n in range(8)]
        XT, XNT, Q, K, VO, S, PT, Y = bank
        OT, TNT = XT, PT
        LG = Y[:, 0:TPC * E]
        DN = S[:, 0:TPC]

        def by_tile(b):
            return b[:, :].rearrange("p (j n) -> p j n", j=TPC)

        w_in = sem("w_in"); e_in = sem("e_in"); e_hi = sem("e_hi"); e_lo = sem("e_lo")
        x_in = [sem(f"x_in{n}") for n in range(GROUPS + 2)]
        pool_c = sem("pool_c"); vec = sem("vec")
        wt_ps = sem("wt_ps"); wt_sb = sem("wt_sb"); wvo_ps = sem("wvo_ps"); wvo_sb = sem("wvo_sb")
        xw_ok = sem("xw_ok")
        xt_ps = sem("xt_ps"); x_ok = sem("x_ok")
        stats = sem("stats"); xn_ok = sem("xn_ok")
        xnt_ps = sem("xnt_ps"); xnt_ok = sem("xnt_ok")
        q_ps = sem("q_ps"); k_ps = sem("k_ps"); vo_ps = sem("vo_ps")
        qk_ok = sem("qk_ok"); vo_ok = sem("vo_ok")
        s_ps = sem("s_ps"); sc_ok = sem("sc_ok"); p_ok = sem("p_ok")
        pt_ps = sem("pt_ps"); pt_ok = sem("pt_ok")
        dn_ps = sem("dn_ps"); y_ps = sem("y_ps"); den_ok = sem("den_ok"); t_ok = sem("t_ok")
        tn_act = sem("tn_act"); tn_ok = sem("tn_ok"); tn_out = sem("tn_out")
        tnt_ps = sem("tnt_ps"); tnt_ok = sem("tnt_ok")
        lg_ps = sem("lg_ps"); lg_ok = sem("lg_ok")
        both_ok = sem("both_ok"); rank_ps = sem("rank_ps"); cnt_ok = sem("cnt_ok"); dm_ok = sem("dm_ok")
        ex_ok = sem("ex_ok"); silu_in = sem("silu_in"); exp_ok = sem("exp_ok"); src_ok = sem("src_ok")
        sel_ok = sem("sel_ok"); sel_used = sem("sel_used")
        gidx_ok = sem("gidx_ok"); xg_in = [sem(f"xg_in{u}") for u in range(RING)]
        xgt_ps = sem("xgt_ps"); xgt_ok = sem("xgt_ok"); xlo_ok = sem("xlo_ok")
        h_ps = sem("h_ps"); sil_ok = sem("sil_ok"); hid_ok = sem("hid_ok")
        ht_ps = sem("ht_ps"); ht_ok = sem("ht_ok"); ye_ps = sem("ye_ps"); ye_ok = sem("ye_ok")
        y_out = sem("y_out")
        cidx_ok = sem("cidx_ok"); yg_in = [sem(f"yg_in{j}") for j in range(TPC)]
        o_ok = sem("o_ok"); o1_ok = sem("o1_ok")
        ot_ps = sem("ot_ps"); ot_half = sem("ot_half"); ot_ok = sem("ot_ok"); o_out = sem("o_out")
        NCONST = 14

        block = ctx.enter_context(nc.Block())

        def wait_apart(eng, *waits):
            waits = [(s, v if isinstance(v, int) else eng.to_reg(v)) for s, v in waits]
            eng.wait_ge(pool_c, NCONST)
            for s, v in waits:
                eng.wait_ge(s, v)

        def wait_past(eng, s, v):
            if not (isinstance(v, int) and v <= 0):
                eng.wait_ge(s, v)

        def by_window(a):
            return a.rearrange("c a (s h w k) -> c (a s) w h k", h=WS, w=W // WS, k=WS)

        def conv_steps(eng, g, step, ticks=None):
            def at(i, k):
                return k <= i < NCH + k
            lo = LAG if g > 0 or ticks is not None else LAG + 1
            for i in range(STEPS):
                if i < lo or i >= NCH - 1:
                    step(i, g * NCH + i, [at(i, k) for k in range(LAG + 1)], g > 0 and at(i, 1), g > 0 and at(i, 2))
                elif i == lo:
                    looped(eng, lo, NCH - 1, lambda i: step(i, g * NCH + i, [True] * (LAG + 1), g > 0, g > 0), ticks)

        def ahead(i, live):
            return live[0] and not (isinstance(i, int) and i == NCH - 1)

        def looped(eng, lo, hi, body, ticks=None):
            if ticks is None:
                with eng.Fori(lo, hi) as i:
                    body(i)
                return
            ticks.base, ticks.count = ticks.now(), 0
            start = ticks.base
            body(lo)
            per = ticks.count
            with eng.Fori(lo + 1, hi) as i:
                ticks.base, ticks.count = (i - lo) * per + start, 0
                body(i)
                assert ticks.count == per
            ticks.base, ticks.count = start + per * (hi - lo), 0

        @block.sync
        def _(sp):
            x_v = x.rearrange("b c (s h) w -> c b s (h w)", s=SPB)
            x_s = x_sb[:, :, :].rearrange("c (b s) t -> c b s t", s=SPB)
            out_v = out.rearrange("b c (s h) w -> c b s (h w)", s=SPB)
            sp.dma_start(x_s[:, 0, 0, :], x_v[:, 0, 0, :]).then_inc(x_in[0], 16)
            for n, w in enumerate((wq, wk, wo, wv)):
                sp.dma_start(raw[:, n, :], w).then_inc(w_in, 16)
            sp.dma_start(bo_row[:, :], bo.rearrange("(a c) -> a c", a=1)).then_inc(w_in, 16)
            for n, b in enumerate((bq, bk, bv)):
                sp.dma_start(bcols[:, n:n + 1], b.rearrange("(c a) -> c a", a=1)).then_inc(w_in, 16)
            sp.dma_start(x_s[:, 0, 1:SPB, :], x_v[:, 0, 1:SPB, :]).then_inc(x_in[1], 16)
            sp.dma_start(wg_sb[:, :], wg).then_inc(w_in, 16)
            half = B // GROUPS
            sp.dma_start(x_s[:, 1:half, :, :].rearrange("c b s t -> c b (s t)"),
                         x_v[:, 1:half, :, :].rearrange("c b s t -> c b (s t)")).then_inc(x_in[2], 16)
            for g in range(1, GROUPS):
                sp.dma_start(x_s[:, g * half:(g + 1) * half, :, :].rearrange("c b s t -> c b (s t)"),
                             x_v[:, g * half:(g + 1) * half, :, :].rearrange("c b s t -> c b (s t)")
                             ).then_inc(x_in[g + 2], 16)
            sp.dma_start(w01[:, :, 0:M], w0.rearrange("e d m -> d e m")).then_inc(e_in, 16)
            sp.dma_start(w01[:, :, M:2 * M], w1.rearrange("e d m -> d e m")).then_inc(e_in, 16)
            for k in range(2):
                sp.dma_start(w2_sb[:, :, k * D:(k + 1) * D],
                             w2[:, k * P:(k + 1) * P, :].rearrange("e m d -> m e d")).then_inc(e_in, 16)

            def tn_store(g, n):
                sp.wait_ge(tn_act, n + 1)
                sp.wait_ge(tn_ok, n + 1)
                rows = tn_dram[g].rearrange("(n j p) d -> p n j d", p=P, j=TPC)
                sp.dma_start(rows[:, bass.ds(n - g * NCH, 1), :, :], tn_sb[:, :, :].unsqueeze(1)).then_inc(tn_out, 16)

            def out_store(n):
                wait_apart(sp, (ot_ok, n + 1))
                dst = out.rearrange("b c (s h) w -> c b s (h w)", s=SPB)
                sp.dma_start(dst[:, bass.ds(n // SPB, 1), bass.ds(n % SPB, 1), :],
                             x_sb[:, bass.ds(n, 1), :].unsqueeze(1)).then_inc(o_out, 16)

            def step(g):
                def run(i, n, live, back, turn):
                    if turn:
                        out_store(n - NCH - 2)
                    if live[3]:
                        tn_store(g, n - 3)
                return run

            def y_store(g, r, half):
                n = (g * ROUNDS + r) * 2 + half
                sp.wait_ge(ye_ok, (n + 1) * HALF)
                rows = y_dram[g].rearrange("(r a u p) d -> p r a u d", p=P, a=2, u=HALF)
                sp.dma_start(rows[:, bass.ds(r, 1), half, :, :], ys[:, half:half + 1, :, :]).then_inc(y_out, 16)
                wait_apart(sp, (y_out, (n + 1) * 16))

            def y_round(g):
                def run(r):
                    y_store(g, r, 0)
                    y_store(g, r, 1)
                return run

            for g in range(GROUPS):
                conv_steps(sp, g, step(g))
                looped(sp, 0, ROUNDS, y_round(g))
            looped(sp, (GROUPS - 1) * NCH, GROUPS * NCH, out_store)
            sp.wait_ge(tn_out, GROUPS * NCH * 16)
            sp.wait_ge(y_out, GROUPS * ROUNDS * 32)
            sp.wait_ge(o_out, GROUPS * NCH * 16)

        @block.gpsimd
        def _(pool):
            made = Ticks()

            def make(ins):
                ins.then_inc(pool_c, 1)
                made.up()

            def count(dst, pattern, base_=0, per_partition=0):
                make(pool.iota(dst, pattern, base=base_, channel_multiplier=per_partition,
                               allow_small_or_imprecise_dtypes=True))

            make(pool.memset(ident[:, :], 0.0))
            make(pool.memset(ones_f[:, :], 1.0))
            make(pool.memset(ones_b[:, :], 1.0))
            make(pool.memset(earlier[:, :, :], 1.0))
            make(pool.memset(ones_row[:, :], 1.0))
            make(pool.memset(inside[:, :, :], 1.0))
            make(pool.memset(eps[:, 0, :], LN_C_EPS))
            make(pool.memset(eps[:, 1, :], LN_T_EPS))
            pool.wait_ge(pool_c, made.now())
            make(pool.affine_select(out=ident[:, :], in_=ident[:, :], compare_op=ALU.not_equal, fill=1.0,
                                    base=0, pattern=[[-1, P]], channel_multiplier=1))
            make(pool.affine_select(out=before_b[:, :], in_=ones_b[:, :], compare_op=ALU.is_gt, fill=0.0,
                                    base=0, pattern=[[1, P]], channel_multiplier=-1))
            make(pool.affine_select(out=earlier[:, :, :], in_=earlier[:, :, :], compare_op=ALU.is_gt, fill=0.0,
                                    base=0, pattern=[[1, E], [-1, E]], channel_multiplier=0))
            make(pool.affine_select(out=inside[:, :, :], in_=inside[:, :, :], compare_op=ALU.is_gt, fill=0.0,
                                    base=0, pattern=[[0, E], [1, NT]], channel_multiplier=0))
            count(token_id[:, :], [[P, NT]], base_=-MID, per_partition=1)
            count(iota_e[:, :], [[1, E]])
            assert made.now() == NCONST
            count(iota_p[:, :], [[1, P]])
            count(iota_t[:, :], [[1, TILES]])
            count(iota_te[:, :, :], [[1, TILES], [0, E]])

            def gather_half(g, r, half, opening=False):
                n = g * ROUNDS + r
                us = range(half * HALF, (half + 1) * HALF)
                if not opening:
                    for u in us:
                        pool.wait_ge(xg_in[u], n * 16)
                pool.tensor_copy(gidx[:, half, :],
                                 src_i[:, bass.ds(r * RING + half * HALF, HALF)]).then_inc(gidx_ok, 1)
                for u in us:
                    free = [] if opening else [(xgt_ps, (n - 1) * RING + u + 1)]
                    wait_apart(pool, (gidx_ok, n * 2 + half + 1), *free)
                    pool.indirect_dma_start(
                        out=xg[:, u, :], out_offset=None, in_=tn_dram[g],
                        in_offset=bass.IndirectOffsetOnAxis(ap=gidx[:, half, u % HALF:u % HALF + 1], axis=0)
                    ).then_inc(xg_in[u], 16)

            def gather_round(g):
                def run(r, opening=False):
                    gather_half(g, r, 0, opening)
                    gather_half(g, r, 1, opening)
                return run

            def back_slots(g, i, b):
                n = g * NCH + i
                for j in range(TPC):
                    wait_past(pool, yg_in[j], (n - 1) * 32)
                pool.tensor_copy(cidx[:, b, :, :], slot_i[:, g, bass.ds(i * TPC, TPC), :]).then_inc(cidx_ok, 1)

            def gather_back(g, i, b, more=True):
                n = g * NCH + i
                for half in range(2):
                    if half == 1 and more:
                        back_slots(g, i + 1, 1 - b)
                    used = (n - 1) * 2 + half + 1
                    free = [] if isinstance(n, int) and n == 0 else [(o_ok, used), (o1_ok, used)]
                    wait_apart(pool, (cidx_ok, n + 1), *free)
                    for j in (half * 2, half * 2 + 1):
                        for k in range(2):
                            pool.indirect_dma_start(
                                out=yg[:, j, k, :], out_offset=None, in_=y_dram[g],
                                in_offset=bass.IndirectOffsetOnAxis(ap=cidx[:, b, j, k:k + 1], axis=0)
                            ).then_inc(yg_in[j], 16)

            def gather_back_two(g):
                def run(i2, last=False):
                    gather_back(g, i2 * 2, 0)
                    gather_back(g, i2 * 2 + 1, 1, more=not last)
                return run

            pool.wait_ge(e_in, 4 * 16)
            pool.tensor_copy(w_hi[:, :, :], w01[:, :, :]).then_inc(e_hi, 1)
            pool.wait_ge(e_hi, 1)
            pool.tensor_tensor(w_lo, w01[:, :, :], w_hi[:, :, :].bitcast(F32), ALU.subtract).then_inc(e_lo, 1)

            for g in range(GROUPS):
                pool.wait_ge(src_ok, g + 1)
                pool.wait_ge(tn_out, (g + 1) * NCH * 16)
                gather_round(g)(0, opening=(g == 0))
                looped(pool, 1, ROUNDS, gather_round(g))
                pool.wait_ge(y_out, (g + 1) * ROUNDS * 32)
                back_slots(g, 0, 0)
                gather_back_two(g)(0)
                looped(pool, 1, NCH // 2 - 1, gather_back_two(g))
                gather_back_two(g)(NCH // 2 - 1, last=True)

        @block.tensor
        def _(pe):
            def transposes(dst, srcs, ready):
                for j, s in enumerate(srcs):
                    mm = pe.transpose(dst[:, j * P:(j + 1) * P], s, ident[:, :])
                mm.then_inc(ready, 1)

            tiles = [slice(j * P, (j + 1) * P) for j in range(TPC)]

            pe.wait_ge(pool_c, NCONST)

            def weights():
                pe.wait_ge(w_in, 9 * 16)
                transposes(Q, [raw[:, n, :] for n in range(3)], wt_ps)
                pe.wait_ge(wt_sb, 2)
                pe.matmul(K[:, 0:P], raw[:, 3, :], woT[:, :], start=True, stop=True)
                pe.matmul(K[:, P:2 * P], bv_b[:, :], woT[:, :], start=True, stop=False)
                pe.matmul(K[:, P:2 * P], ones_row[:, :], bo_row[:, :], start=False, stop=True).then_inc(wvo_ps, 1)
                pe.wait_ge(wvo_sb, 4)

            def step(g):
                def run(i, n, live, back, turn):
                    if g == 0 and isinstance(i, int) and i == 1:
                        weights()
                    if live[1]:
                        pe.wait_ge(xn_ok, n)
                        wait_past(pe, xnt_ok, n - 1)
                        transposes(XNT, [xn[:, j, :] for j in range(TPC)], xnt_ps)
                    if live[4]:
                        pe.wait_ge(tnt_ok, n - 3)
                        pe.wait_ge(t_ok, n - 2 if live[3] else (g + 1) * NCH)
                        wait_past(pe, lg_ok, n - 4)
                        for j, t in enumerate(tiles):
                            mm = pe.matmul(LG[:, j * E:(j + 1) * E], tnT[:, t], wg_sb[:, :], start=True, stop=True)
                        mm.then_inc(lg_ps, 1)
                    if live[1]:
                        pe.wait_ge(xnt_ok, n)
                        wait_past(pe, qk_ok, 2 * (n - 1))
                        pe.matmul(Q[:, :], wqT[:, :], xnT[:, :], start=True, stop=True).then_inc(q_ps, 1)
                    if live[2]:
                        pe.wait_ge(p_ok, n - 1)
                        wait_past(pe, tnt_ok, n - 3)
                        transposes(PT, [prob[:, j, :] for j in range(TPC)], pt_ps)
                    if live[1]:
                        pe.matmul(K[:, :], wkT[:, :], xnT[:, :], start=True, stop=True).then_inc(k_ps, 1)
                    if turn:
                        pe.wait_ge(x_ok, n + 1 if live[0] else (g + 1) * NCH)
                        turn_back(n - NCH - 2)
                    if live[2]:
                        pe.wait_ge(pt_ok, n - 1)
                        for j, t in enumerate(tiles):
                            mm = pe.matmul(DN[:, j:j + 1], pT[:, t], ones_f[:, 0:1], start=True, stop=True)
                        mm.then_inc(dn_ps, 1)
                        pe.wait_ge(vo_ok, n - 1)
                        wait_past(pe, lg_ok, n - 3)
                        for j, t in enumerate(tiles):
                            mm = pe.matmul(Y[:, t], pT[:, t], vo_sb[:, j, :], start=True, stop=True)
                        mm.then_inc(y_ps, 1)
                    if live[1]:
                        wait_past(pe, vo_ok, n - 1)
                        pe.matmul(VO[:, :], ones_r[:, :], bvo_hi[:, :], start=True, stop=False)
                        pe.matmul(VO[:, :], ones_r[:, :], bvo_lo[:, :], start=False, stop=False)
                        for t in tiles:
                            mm = pe.matmul(VO[:, t], xnT[:, t], wvo[:, :], start=False, stop=(t is tiles[-1]))
                        mm.then_inc(vo_ps, 1)
                    if live[1]:
                        pe.wait_ge(qk_ok, 2 * n)
                        wait_past(pe, den_ok, n - 1)
                        for t in tiles:
                            mm = pe.matmul(S[:, t], q_sb[:, t], k_sb[:, t], start=True, stop=True)
                        mm.then_inc(s_ps, 1)
                    if ahead(i, live):
                        pe.wait_ge(x_ok, n + 1)
                        if g > 0:
                            wait_past(pe, ot_ok, (g - 1) * NCH + i - 1)
                        token_rows(n + 1)
                    if live[3]:
                        pe.wait_ge(tn_act, n - 2)
                        pe.wait_ge(tn_ok, n - 2)
                        pe.wait_ge(pt_ok, n - 1 if live[2] else (g + 1) * NCH)
                        transposes(TNT, [tn_sb[:, j, :] for j in range(TPC)], tnt_ps)
                return run

            def token_rows(n):
                pe.wait_ge(xw_ok, 2 * (n + 1))
                transposes(XT, [xw[:, t] for t in tiles], xt_ps)

            def turn_back(n):
                pe.wait_ge(o_ok, 2 * (n + 1))
                pe.wait_ge(o1_ok, 2 * (n + 1))
                for j, t in enumerate(tiles):
                    pe.matmul(OT[:, t], o2[:, j, :], ident[:, :], start=True, stop=False)
                    mm = pe.matmul(OT[:, t], o1[:, j, :], ident[:, :], start=False, stop=True)
                mm.then_inc(ot_ps, 1)

            hi_v = w_hi[:, :, :].rearrange("p e n -> p (e n)")
            lo_v = w_lo.rearrange("p e n -> p (e n)")
            w2_v = w2_sb[:, :, :].rearrange("p e n -> p (e n)")

            expert_of = [pe.alloc_register(f"expert_of_tile{u}_{k}") for u in range(RING) for k in range(2)]

            def load_experts(r, half):
                pe.load(expert_of[half * RING:(half + 1) * RING],
                        exp_at[0:1, bass.ds(r * RING + half * HALF, HALF), :].rearrange("p u k -> p (u k)"))

            def expert(u, k):
                return pe.snap(expert_of[u % RING * 2 + k], min_val=0, max_val=(E - 1) * 2 * M // (k + 1))

            def expert_round(g, r, start=False, end=False):
                n0 = (g * ROUNDS + r) * RING

                def turn_x(u):
                    n = n0 + u
                    pe.wait_ge(xg_in[u % RING], (g * ROUNDS + r + u // RING + 1) * 16)
                    wait_past(pe, xlo_ok, n - 1)
                    pe.transpose(bank[u % 2][:, 0:P], xg[:, u % RING, :], ident[:, :]).then_inc(xgt_ps, 1)

                def hidden(u, at):
                    n = n0 + u
                    pe.wait_ge(xgt_ok, n + 1)
                    wait_past(pe, hid_ok, n - 1)
                    h, x, w = bank[2 + u % 2][:, :], u % 2, bass.ds(at, 2 * M)
                    pe.matmul(h, x_hi[:, x, :], hi_v[:, w], start=True, stop=False)
                    pe.matmul(h, x_hi[:, x, :], lo_v[:, w], start=False, stop=False)
                    pe.wait_ge(xlo_ok, n + 1)
                    pe.matmul(h, x_lo[:, x, :], hi_v[:, w], start=False, stop=True).then_inc(h_ps, 1)

                def turn_h(u):
                    n = n0 + u
                    pe.wait_ge(hid_ok, n + 1)
                    wait_past(pe, ht_ok, n - 1)
                    pe.transpose(bank[4 + u % 2][:, 0:P], hid[:, u % 2, 0:P], ident[:, :])
                    pe.transpose(bank[4 + u % 2][:, P:M], hid[:, u % 2, P:M], ident[:, :]).then_inc(ht_ps, 1)

                def down(u, at):
                    n = n0 + u
                    pe.wait_ge(ht_ok, n + 1)
                    wait_past(pe, ye_ok, n - 1)
                    pe.matmul(bank[6 + u % 2][:, 0:D], hT[:, u % 2, 0:P], w2_v[:, bass.ds(at, D)],
                              start=True, stop=False)
                    pe.matmul(bank[6 + u % 2][:, 0:D], hT[:, u % 2, P:M], w2_v[:, D:][:, bass.ds(at, D)],
                              start=False, stop=True).then_inc(ye_ps, 1)

                if start:
                    load_experts(r, 0)
                    turn_x(0)
                for u in range(RING):
                    if not (end and u == RING - 1):
                        turn_x(u + 1)
                    hidden(u, expert(u, 0))
                    if u == 2:
                        load_experts(r, 1)
                    if u == HALF + 2 and not end:
                        load_experts(r + 1, 0)
                    if not (start and u < 2):
                        down(u - 2, expert(u - 2, 1))
                    if not (start and u < 1):
                        turn_h(u - 1)
                if end:
                    down(RING - 2, expert(RING - 2, 1))
                    turn_h(RING - 1)
                    down(RING - 1, expert(RING - 1, 1))

            for g in range(GROUPS):
                token_rows(g * NCH)
                conv_steps(pe, g, step(g))
                pe.wait_ge(qk_ok, 2 * (g + 1) * NCH)
                pe.wait_ge(both_ok, g + 1)
                both_v = both[:, :, :].rearrange("p j e -> p (j e)")
                pe.matmul(K[:, :], ones_b[:, :], both_v, start=True, stop=True)
                pe.matmul(Q[:, :], before_b[:, :], both_v, start=True, stop=True).then_inc(rank_ps, 1)
                pe.wait_ge(cnt_ok, g + 1)

                def pick(i, b, first_=False, last=False):
                    pe.wait_ge(sel_ok, g * NT // 2 + i + 1)
                    for j in range(2):
                        for k in range(2):
                            mm = pe.matmul(K[:, 0:TILES], sel_p[:, b, j, k, :], sel_t[:, b, j, k, :],
                                           start=(first_ and j == k == 0), stop=(last and j == k == 1))
                    mm.then_inc(sel_used, 1)

                def picks(i2):
                    pick(i2 * 2, 0)
                    pick(i2 * 2 + 1, 1)
                pick(0, 0, first_=True)
                pick(1, 1)
                looped(pe, 1, NT // 4 - 1, picks)
                pick(NT // 2 - 2, 0)
                pick(NT // 2 - 1, 1, last=True)
                pe.wait_ge(src_ok, g + 1)
                if g == 0:
                    pe.wait_ge(e_in, 4 * 16)
                    pe.wait_ge(e_lo, 1)
                pe.wait_ge(exp_ok, 2 * (g + 1))
                if g > 0:
                    pe.wait_ge(ot_ok, g * NCH)
                expert_round(g, 0, start=True)
                looped(pe, 1, ROUNDS - 1, lambda r: expert_round(g, r))
                expert_round(g, ROUNDS - 1, end=True)
                pe.wait_ge(ye_ok, (g + 1) * TILES)

            def last_turn(n):
                pe.wait_ge(ot_ok, n)
                turn_back(n)
            looped(pe, (GROUPS - 1) * NCH, GROUPS * NCH, last_turn)

        @block.scalar
        def _(act):
            def out_copy(n):
                act.wait_ge(ot_ps, n + 1)
                dst = by_window(x_sb[:, bass.ds(n, 1), :])
                src = OT[:, :].rearrange("c (s w h k) -> c s w h k", s=CHUNK // W // WS, h=WS, k=WS)
                act.copy(dst[:, 0, :, :, :], src[:, 0, :, :, :]).then_inc(ot_half, 1)
                act.copy(dst[:, 1, :, :, :], src[:, 1, :, :, :]).then_inc(ot_ok, 1)

            def window_order(n):
                src = by_window(x_sb[:, bass.ds(n, 1), :])
                dst = xw[:, :].rearrange("c (s w h k) -> c s w h k", w=W // WS, h=WS, k=WS)
                for s in range(2):
                    act.copy(dst[:, s, :, :, :], src[:, s, :, :, :]).then_inc(xw_ok, 1)

            def first_rows(n, half):
                js = (half * 2, half * 2 + 1)
                used = [] if isinstance(n, int) and n == 0 else [(ot_ps, n)]
                wait_apart(act, *[(yg_in[j], (n + 1) * 32) for j in js], *used)
                for j in js:
                    ins = act.activation(o1[:, j, :], yg[:, j, 0, :], ACT.Copy,
                                         scale=gate[:, 0, bass.ds(n * TPC + j, 1)])
                ins.then_inc(o1_ok, 1)

            def x_rows(n):
                act.wait_ge(xt_ps, n + 1)
                act.copy(t_sb[:, bass.ds(n * TPC, TPC), :], by_tile(XT)).then_inc(x_ok, 1)

            def step(g):
                def run(i, n, live, back, turn):
                    if live[1]:
                        act.wait_ge(xnt_ps, n)
                        wait_past(act, vo_ps, n - 1)
                        act.copy(xnT[:, :], XNT[:, :]).then_inc(xnt_ok, 1)
                    if live[0]:
                        x_rows(n)
                    if live[2]:
                        act.wait_ge(sc_ok, n - 1)
                        wait_past(act, pt_ps, n - 2)
                        h = P // 2
                        act.activation(prob[0:h, :, 0:h], sc[0:h, :, :], ACT.Exp, scale=SCALE)
                        act.activation(prob[h:P, :, h:P], sc[h:P, :, :], ACT.Exp, scale=SCALE).then_inc(p_ok, 1)
                    if live[1]:
                        act.wait_ge(q_ps, n)
                        wait_past(act, s_ps, n - 1)
                        act.activation(q_sb[:, :], Q[:, :], ACT.Identity, bias=bcols[:, 0:1]).then_inc(qk_ok, 1)
                    if live[2]:
                        act.wait_ge(pt_ps, n - 1)
                        wait_past(act, y_ps, n - 2)
                        act.copy(pT[:, :], PT[:, :]).then_inc(pt_ok, 1)
                    if live[1]:
                        act.wait_ge(k_ps, n)
                        act.activation(k_sb[:, :], K[:, :], ACT.Identity, bias=bcols[:, 1:2]).then_inc(qk_ok, 1)
                    if turn:
                        out_copy(n - NCH - 2)
                    if back:
                        first_rows(n - NCH - 1, 0)
                    if ahead(i, live):
                        if g == 0 and isinstance(i, int) and i < 2:
                            act.wait_ge(x_in[i + 1], 16)
                        act.wait_ge(xt_ps, n + 1)
                        window_order(n + 1)
                    if live[3]:
                        m = n - 3
                        used = [] if isinstance(m, int) and m == 0 else [(tnt_ps, m), (tn_out, m * 16)]
                        wait_apart(act, (stats, g * (STEPS - 1) + i + 1), *used)
                        normed(tn_sb, m, 1, TN_ACT[g]).then_inc(tn_act, 1)
                    if live[0]:
                        used = [] if isinstance(n, int) and n == 0 else [(xnt_ps, n)]
                        wait_apart(act, (stats, g * (STEPS - 1) + i + 1), *used)
                        normed(xn, n, 0, TPC).then_inc(xn_ok, 1)
                    if live[1]:
                        act.wait_ge(vo_ps, n)
                        wait_past(act, y_ps, n - 1)
                        act.copy(vo_sb[:, :, :], by_tile(VO)).then_inc(vo_ok, 1)
                    if live[3]:
                        act.wait_ge(tnt_ps, n - 2)
                        wait_past(act, lg_ps, n - 3)
                        act.copy(tnT[:, :], TNT[:, :]).then_inc(tnt_ok, 1)
                    if back:
                        first_rows(n - NCH - 1, 1)
                return run

            def normed(dst, n, k, tiles):
                for j in range(tiles):
                    rows = t_sb[:, bass.ds(n * TPC + j, 1), :].rearrange("p a d -> p (a d)")
                    ins = act.activation(dst[:, j, :], rows, ACT.Identity, bias=nb[:, k, j:j + 1],
                                         scale=rs[:, k, j:j + 1])
                return ins

            def x_copy(n0, u):
                n = n0 + u
                act.wait_ge(xgt_ps, n + 1)
                wait_past(act, h_ps, n - 1)
                act.copy(x_hi[:, u % 2, :], bank[u % 2][:, 0:P]).then_inc(xgt_ok, 1)

            def silu(n0, u):
                n = n0 + u
                act.wait_ge(h_ps, n + 1)
                wait_past(act, hid_ok, n - 1)
                act.activation(sil[:, u % 2, :], bank[2 + u % 2][:, 0:M], ACT.Silu).then_inc(sil_ok, 1)

            def expert_round(g, r, start=False, end=False):
                n0 = (g * ROUNDS + r) * RING
                if start:
                    x_copy(n0, 0)
                for u in range(RING):
                    if not (end and u == RING - 1):
                        x_copy(n0, u + 1)
                    silu(n0, u)

            act.wait_ge(x_in[0], 16)
            window_order(0)
            for g in range(GROUPS):
                if g > 0:
                    act.wait_ge(x_in[g + 2], 16)
                    window_order(g * NCH)
                conv_steps(act, g, step(g))
                act.wait_ge(dm_ok, g + 1)
                act.activation(ex[:, :], dm[:, :], ACT.Exp).then_inc(ex_ok, 1)
                act.wait_ge(rank_ps, g + 1)
                act.copy(cnt[:, :, :].rearrange("p e j -> p j e"),
                         K[:, :].rearrange("p (j e) -> p j e", e=E)).then_inc(cnt_ok, 1)
                act.activation(silu_try[:, :], ones_f[:, 0:1], ACT.Silu).then_inc(silu_in, 1)
                act.wait_ge(silu_in, g + 1)
                expert_round(g, 0, start=True)
                looped(act, 1, ROUNDS - 1, lambda r: expert_round(g, r))
                expert_round(g, ROUNDS - 1, end=True)

            def last_rows(n):
                first_rows(n, 0)
                first_rows(n, 1)
                out_copy(n)
            looped(act, (GROUPS - 1) * NCH, GROUPS * NCH, last_rows)

        @block.vector
        def _(dve):
            tick = Ticks()

            def then(ins):
                ins.then_inc(vec, 1)
                tick.up()

            def settled():
                dve.wait_ge(vec, tick.now())

            def chain(ins):
                then(ins)
                settled()

            dve.wait_ge(pool_c, NCONST)
            then(dve.memset(prob[:, :, :], 0.0))

            def weights():
                dve.wait_ge(w_in, 9 * 16)
                dve.tensor_copy(bv_b[:, :], bcols[:, 2:3].to_broadcast([P, P])).then_inc(wt_sb, 1)
                dve.wait_ge(wt_ps, 1)
                dve.tensor_copy(woT[:, :], Q[:, 2 * P:3 * P]).then_inc(wt_sb, 1)
                dve.tensor_copy(wqT[:, :], Q[:, 0:P]).then_inc(wvo_sb, 1)
                dve.tensor_copy(wkT[:, :], Q[:, P:2 * P]).then_inc(wvo_sb, 1)
                dve.wait_ge(wvo_ps, 1)
                dve.tensor_copy(wvo[:, :], K[:, 0:P]).then_inc(wvo_sb, 1)
                hi, lo = (b[:, :].rearrange("a (j c) -> a j c", j=TPC) for b in (bvo_hi, bvo_lo))
                row = K[0:1, P:2 * P].unsqueeze(1).to_broadcast([1, TPC, P])
                chain(dve.tensor_copy(hi, row))
                then(dve.tensor_copy(ones_r[:, :], ones_row[:, :]))
                dve.tensor_tensor(lo, row, hi.bitcast(F32), ALU.subtract).then_inc(wvo_sb, 1)
                dve.wait_ge(wvo_sb, 4)
                settled()

            def moments(rows, k):
                for j in range(TPC):
                    then(dve.bn_stats(st[:, k, j, :], rows[j]))

            def aggregate(ks):
                wait_apart(dve, (vec, tick.now()))
                for k in ks:
                    for j in range(TPC):
                        then(dve.bn_aggr(mv[:, k, j, :], st[:, k, j, :]))

            def largest(j):
                then(dve.max(best[:, j, :], LG[:, j * E:(j + 1) * E]))

            def places(j):
                ins = dve.max_index(best_i[:, j, :], best[:, j, :], LG[:, j * E:(j + 1) * E])
                if j < TPC - 1:
                    then(ins)
                else:
                    ins.then_inc(lg_ok, 1)

            def keep(i, dst, src):
                then(dve.tensor_copy(dst[:, bass.ds(i * TPC, TPC), :], src[:, :, 0:2]))

            def roots(k, ranked):
                done_ = 0

                def link(ins):
                    nonlocal done_
                    then(ins)
                    mine = tick.now()
                    if ranked is not None:
                        if done_ < TPC:
                            largest(done_)
                        elif done_ < 2 * TPC:
                            places(done_ - TPC)
                        elif done_ == 2 * TPC:
                            keep(ranked, top_v, best)
                    done_ += 1
                    dve.wait_ge(vec, mine)
                link(dve.tensor_tensor(var[:, k, :], mv[:, k, :, 1], eps[:, k, :], ALU.add))
                link(dve.tensor_scalar(bits[:, k, :], var[:, k, :].bitcast(I32), 1, None, ALU.logical_shift_right))
                link(dve.tensor_scalar(rs[:, k, :].bitcast(I32), bits[:, k, :], -1.0, float(0x5f3759df),
                                       ALU.mult, ALU.add))
                for _ in range(3):
                    link(dve.tensor_tensor(sq[:, k, :], rs[:, k, :], rs[:, k, :], ALU.mult))
                    link(dve.scalar_tensor_tensor(out=sq[:, k, :], in0=sq[:, k, :], scalar=-0.5, in1=var[:, k, :],
                                                  op0=ALU.mult, op1=ALU.mult))
                    link(dve.scalar_tensor_tensor(out=rs[:, k, :], in0=sq[:, k, :], scalar=1.5, in1=rs[:, k, :],
                                                  op0=ALU.add, op1=ALU.mult))
                dve.scalar_tensor_tensor(out=nb[:, k, :], in0=mv[:, k, :, 0], scalar=-1.0, in1=rs[:, k, :],
                                         op0=ALU.mult, op1=ALU.mult).then_inc(stats, 1)

            def token_rows(n, j):
                return t_sb[:, bass.ds(n * TPC + j, 1), :].rearrange("p a d -> p (a d)")

            def combine(n, half):
                js = (half * 2, half * 2 + 1)
                for j in js:
                    dve.wait_ge(yg_in[j], (n + 1) * 32)
                wait_past(dve, ot_ps, n)
                for j in js:
                    ins = dve.scalar_tensor_tensor(out=o2[:, j, :], in0=yg[:, j, 1, :],
                                                   scalar=gate[:, 1, bass.ds(n * TPC + j, 1)],
                                                   in1=token_rows(n, j), op0=ALU.mult, op1=ALU.add)
                    if j == js[0]:
                        then(ins)
                ins.then_inc(o_ok, 1)

            def step(g):
                def run(i, n, live, back, turn):
                    if g == 0 and isinstance(i, int) and i == 1:
                        weights()
                    if live[2]:
                        dve.wait_ge(s_ps, n - 1)
                        h = P // 2
                        sv = by_tile(S)
                        then(dve.tensor_reduce(smax[0:h, :], sv[0:h, :, 0:h], AX.X, ALU.max))
                        then(dve.tensor_reduce(smax[h:P, :], sv[h:P, :, h:P], AX.X, ALU.max))
                        settled()
                        wait_past(dve, p_ok, n - 2)
                        then(dve.tensor_tensor(sc[0:h, :, :], sv[0:h, :, 0:h],
                                               smax[0:h, :].unsqueeze(2).to_broadcast([h, TPC, h]), ALU.subtract))
                        dve.tensor_tensor(sc[h:P, :, :], sv[h:P, :, h:P],
                                          smax[h:P, :].unsqueeze(2).to_broadcast([h, TPC, h]),
                                          ALU.subtract).then_inc(sc_ok, 1)
                    if live[0]:
                        wait_apart(dve, (x_ok, n + 1))
                        moments([token_rows(n, j) for j in range(TPC)], 0)
                    if live[0] or live[3]:
                        aggregate(([0] if live[0] else []) + ([1] if live[3] else []))
                        settled()
                        wait_past(dve, xn_ok, n if live[0] else (g + 1) * NCH)
                        if live[3]:
                            wait_past(dve, tn_act, n - 3)
                        if live[4]:
                            dve.wait_ge(lg_ps, n - 3)
                        roots(slice(0 if live[0] else 1, 2 if live[3] else 1), i - 4 if live[4] else None)
                    elif live[4]:
                        dve.wait_ge(lg_ps, n - 3)
                        for j in range(TPC):
                            largest(j)
                        settled()
                        for j in range(TPC):
                            places(j)
                        keep(i - 4, top_v, best)
                    if live[4]:
                        dve.wait_ge(lg_ok, n - 3)
                        settled()
                        keep(i - 4, top_e, best_i)
                    if live[2]:
                        dve.wait_ge(dn_ps, n - 1)
                        dve.reciprocal(den[:, :], DN).then_inc(den_ok, 1)
                    if live[3]:
                        m = n - 3
                        wait_past(dve, tnt_ps, m)
                        wait_past(dve, tn_out, m * 16)
                        for j in range(TN_ACT[g], TPC):
                            ins = dve.tensor_scalar(tn_sb[:, j, :], token_rows(m, j), mv[:, 1, j, 0:1],
                                                    rs[:, 1, j:j + 1], ALU.subtract, ALU.mult)
                            if j < TPC - 1:
                                then(ins)
                        ins.then_inc(tn_ok, 1)
                    if back:
                        combine(n - NCH - 1, 0)
                    if live[2]:
                        m = n - 2
                        dve.wait_ge(y_ps, m + 1)
                        dve.wait_ge(den_ok, m + 1)
                        rows = [token_rows(m, j) for j in range(TPC)]
                        for j in range(TPC):
                            ins = dve.scalar_tensor_tensor(out=rows[j], in0=Y[:, tile_cols(j)],
                                                           scalar=den[:, j:j + 1], in1=rows[j],
                                                           op0=ALU.mult, op1=ALU.add)
                            if j < TPC - 1:
                                then(ins)
                        ins.then_inc(t_ok, 1)
                        wait_apart(dve, (t_ok, m + 1), (vec, tick.now()))
                        moments(rows, 1)
                    if back:
                        combine(n - NCH - 1, 1)
                return run

            def tile_cols(j):
                return slice(j * P, (j + 1) * P)

            def route(g):
                settled()
                dve.wait_ge(lg_ok, (g + 1) * NCH)
                for k in range(2):
                    then(dve.tensor_tensor(oh[:, k, :, :], iota_e[:, :].unsqueeze(1).to_broadcast([P, NT, E]),
                                           top_e[:, :, k].unsqueeze(2).to_broadcast([P, NT, E]), ALU.is_equal))
                settled()
                dve.tensor_tensor(both[:, :, :], oh[:, 0, :, :], oh[:, 1, :, :], ALU.add).then_inc(both_ok, 1)
                dve.tensor_tensor(dm[:, :], top_v[:, :, 1], top_v[:, :, 0], ALU.subtract).then_inc(dm_ok, 1)
                dve.wait_ge(ex_ok, g + 1)
                own = slice(g * NT, (g + 1) * NT)
                chain(dve.tensor_scalar(ex1[:, :], ex[:, :], 1.0, None, ALU.add))
                chain(dve.reciprocal(gate[:, 0, own], ex1[:, :]))
                then(dve.tensor_tensor(gate[:, 1, own], gate[:, 0, own], ex[:, :], ALU.mult))
                dve.wait_ge(cnt_ok, g + 1)
                flat = "p e j -> p (e j)"
                chain(dve.tensor_tensor_scan(upto[:, :, :].rearrange(flat), inside[:, :, :].rearrange(flat),
                                             cnt[:, :, :].rearrange(flat), 0.0, ALU.mult, ALU.add))
                chain(dve.tensor_scalar(tot_i[:, :], upto[:, :, NT - 1], float(P - 1), None, ALU.add))
                chain(dve.tensor_scalar(cnt_i[:, :], tot_i[:, :], 7, None, ALU.logical_shift_right))
                chain(dve.tensor_copy(ntile[:, :], cnt_i[:, :]))
                chain(dve.tensor_tensor(prod[:, :, :], earlier[:, :, :],
                                        ntile[:, :].unsqueeze(1).to_broadcast([P, E, E]), ALU.mult))
                chain(dve.tensor_reduce(first[:, :], prod[:, :, :], AX.X, ALU.add))
                then(dve.tensor_tensor(ends[:, :], first[:, :], ntile[:, :], ALU.add))
                then(dve.tensor_scalar(base[:, :], first[:, :], float(P), None, ALU.mult))
                chain(dve.tensor_tensor(upto[:, :, :], upto[:, :, :], cnt[:, :, :], ALU.subtract))
                chain(dve.tensor_tensor(upto[:, :, :], upto[:, :, :],
                                        base[:, :].unsqueeze(2).to_broadcast([P, E, NT]), ALU.add))
                chain(dve.tensor_tensor(place[:, :, :], Q[:, :].rearrange("p (j e) -> p j e", e=E),
                                        upto[:, :, :].rearrange("p e j -> p j e"), ALU.add))
                for k in range(2):
                    then(dve.tensor_tensor(pp[:, k, :, :], place[:, :, :], oh[:, k, :, :], ALU.mult))
                settled()
                chain(dve.tensor_reduce(slot[:, :, :], pp[:, :, :, :], AX.X, ALU.add))
                chain(dve.tensor_copy(slot_i[:, g, :, :].rearrange("p j k -> p k j"), slot[:, :, :]))
                then(dve.tensor_scalar(hi_i[:, :, :], slot_i[:, g, :, :], 7, None, ALU.logical_shift_right))
                chain(dve.tensor_scalar(lo_i[:, :, :], slot_i[:, g, :, :], P - 1, None, ALU.bitwise_and))
                then(dve.tensor_copy(hi_f[:, :, :], hi_i[:, :, :]))
                chain(dve.tensor_copy(lo_f[:, :, :], lo_i[:, :, :]))

                hi_v = hi_f[:, :, :].rearrange("p j k -> p (j k)")

                def pick_rows(i, b):
                    wait_past(dve, sel_used, g * NT // 2 + i - 1)
                    then(dve.tensor_tensor(sel_t[:, b, :, :, :].rearrange("p j k t -> p (j k) t"),
                                           iota_t[:, :].unsqueeze(1).to_broadcast([P, 4, TILES]),
                                           hi_v[:, bass.ds(i * 4, 4)].unsqueeze(2).to_broadcast([P, 4, TILES]),
                                           ALU.is_equal))
                    for j in range(2):
                        col = bass.ds(i * 2 + j, 1)
                        for k in range(2):
                            lo = lo_f[:, col, k:k + 1].rearrange("p a b -> p (a b)")
                            ins = dve.tensor_scalar(sel_p[:, b, j, k, :], iota_p[:, :], lo, token_id[:, col],
                                                    ALU.is_equal, ALU.mult)
                            if not j == k == 1:
                                then(ins)
                    ins.then_inc(sel_ok, 1)

                def pick_two(i2):
                    pick_rows(i2 * 2, 0)
                    pick_rows(i2 * 2 + 1, 1)
                looped(dve, 0, NT // 4, pick_two, tick)
                dve.wait_ge(sel_used, (g + 1) * NT // 2)
                dve.tensor_scalar(src_i[:, :], K[:, 0:TILES], float(MID), None, ALU.add).then_inc(src_ok, 1)
                chain(dve.tensor_tensor(done[:, :, :], iota_te[:, :, :],
                                        ends[:, :].unsqueeze(1).to_broadcast([P, TILES, E]), ALU.is_ge))
                chain(dve.tensor_reduce(exp_f[:, :], done[:, :, :], AX.X, ALU.add))
                chain(dve.tensor_scalar(exp_f[:, :], exp_f[:, :], float(E - 1), None, ALU.min))
                for k in range(2):
                    dve.tensor_scalar(exp_at[:, :, k], exp_f[:, :], float(2 * M // (k + 1)), None,
                                      ALU.mult).then_inc(exp_ok, 1)

            def experts(g):
                def product(n0, u):
                    n = n0 + u
                    dve.wait_ge(sil_ok, n + 1)
                    wait_past(dve, ht_ps, n - 1)
                    dve.tensor_tensor(hid[:, u % 2, :], sil[:, u % 2, :], bank[2 + u % 2][:, M:2 * M],
                                      ALU.mult).then_inc(hid_ok, 1)

                def y_copy(n0, round_, u):
                    n = n0 + u
                    dve.wait_ge(ye_ps, n + 1)
                    half = (u // HALF) % 2
                    if u % HALF == 0:
                        wait_past(dve, y_out, ((round_ - 1) * 2 + half + 1) * 16)
                    dve.tensor_copy(ys[:, half, u % HALF, :], bank[6 + u % 2][:, 0:D]).then_inc(ye_ok, 1)

                def ht_copy(n0, u):
                    n = n0 + u
                    dve.wait_ge(ht_ps, n + 1)
                    wait_past(dve, ye_ps, n - 1)
                    dve.tensor_copy(hT[:, u % 2, :], bank[4 + u % 2][:, 0:M]).then_inc(ht_ok, 1)

                def x_rest(n0, u):
                    n = n0 + u
                    dve.wait_ge(xgt_ok, n + 1)
                    wait_past(dve, h_ps, n - 1)
                    dve.tensor_tensor(x_lo[:, u % 2, :], bank[u % 2][:, 0:P], x_hi[:, u % 2, :].bitcast(F32),
                                      ALU.subtract).then_inc(xlo_ok, 1)

                def one_round(r, start=False, end=False):
                    n0 = (g * ROUNDS + r) * RING
                    if start:
                        x_rest(n0, 0)
                    for u in range(RING):
                        if not (end and u == RING - 1):
                            x_rest(n0, u + 1)
                        product(n0, u)
                        if not (start and u < 1):
                            ht_copy(n0, u - 1)
                        if not (start and u < 2):
                            y_copy(n0, g * ROUNDS + r, u - 2)
                one_round(0, start=True)
                looped(dve, 1, ROUNDS - 1, one_round)
                one_round(ROUNDS - 1, end=True)
                n0 = (g + 1) * TILES
                y_copy(n0, None, -2)
                ht_copy(n0, -1)
                y_copy(n0, None, -1)

            for g in range(GROUPS):
                conv_steps(dve, g, step(g), tick)
                if g == 0:
                    dve.wait_ge(pool_c, NCONST + 3)
                route(g)
                experts(g)

            def last_rows(n):
                combine(n, 0)
                combine(n, 1)
            looped(dve, (GROUPS - 1) * NCH, GROUPS * NCH, last_rows, tick)


_INS = ["x", "L0_conv_wq", "L0_conv_bq", "L0_conv_wk", "L0_conv_bk", "L0_conv_wv", "L0_conv_bv",
        "L0_conv_wo", "L0_conv_bo", "L0_ffn_wg", "L0_ffn_w0", "L0_ffn_w1", "L0_ffn_wo"]


def kernel(**inputs):
    import numpy as _np
    import concourse.bacc as _bacc
    from concourse import mybir as _mybir
    from concourse.bass_utils import run_bass_kernel_spmd as _run

    nc = _bacc.Bacc("TRN2", target_bir_lowering=False, num_devices=1)
    arrays, args = {}, []
    for name in _INS:
        a = _np.ascontiguousarray(inputs[name])
        arrays[f"in_{name}"] = a
        args.append(nc.dram_tensor(f"in_{name}", a.shape, _mybir.dt.from_np(a.dtype), kind="ExternalInput").ap())
    shape = inputs["x"].shape
    out = nc.dram_tensor("out_0", shape, _mybir.dt.from_np(_np.dtype("float32")), kind="ExternalOutput").ap()
    emit(nc, *args, out)
    r = _run(nc, [arrays], core_ids=[0])
    return r.results[0]["out_0"]
```
